# Optimizing a Trainium2 kernel written in Bass

```python
import numpy as np
import jax
import jax.numpy as jnp

def _softmax(x, axis=-1):
    return jax.nn.softmax(x, axis=axis)

def _gelu(x):
    return jax.nn.gelu(x, approximate=True)

def _silu(x):
    return jax.nn.silu(x)

def _sigmoid(x):
    return jax.nn.sigmoid(x)

def _layernorm(x, axis=-1, eps=1e-05):
    m = jnp.mean(x, axis=axis, keepdims=True)
    v = jnp.var(x, axis=axis, keepdims=True)
    return (x - m) / jnp.sqrt(v + eps)

def _scatter_add(tgt, idx, src, axis=0):
    return tgt.at[idx].add(src)

def _segment_sum(src, seg, n):
    return jax.ops.segment_sum(src, seg, n)
kernel_name = 'mk_recurrent_d1_jaxref_r8_95ae8a'

def setup_inputs(seed: int=0):
    np.random.seed(seed)
    _w = jnp.asarray

    def _L0_attn_setup():
        import jax, jax.numpy as jnp
        import numpy as np
        D_MODEL, N_HEADS, LATENT, ROPE = (512, 128, 64, 64)
        HEAD_DIM = D_MODEL // N_HEADS
        B, S = (2, 128)
        key = jax.random.key(seed)
        ks = jax.random.split(key, 9)

        def w(k, i, o):
            return jax.random.normal(k, (i, o), dtype=jnp.float32) * (1.0 / np.sqrt(i))
        return {'x': jax.random.normal(ks[0], (B, S, D_MODEL), dtype=jnp.float32), 'Wq_down': w(ks[1], D_MODEL, LATENT), 'Wq_up': w(ks[2], LATENT, N_HEADS * HEAD_DIM), 'Wq_rope': w(ks[3], D_MODEL, N_HEADS * ROPE), 'Wkv_down': w(ks[4], D_MODEL, LATENT), 'Wk_up': w(ks[5], LATENT, N_HEADS * HEAD_DIM), 'Wv_up': w(ks[6], LATENT, N_HEADS * HEAD_DIM), 'Wk_rope': w(ks[7], D_MODEL, ROPE), 'Wo': w(ks[8], N_HEADS * HEAD_DIM, D_MODEL)}
    _L0_attn_in = _L0_attn_setup()

    def _L0_ffn_setup():
        import jax, jax.numpy as jnp
        import numpy as np
        LORA_SCALING = 1.0 / 2.0

        def _qlora_linear(x, wq, A, B):
            w = jnp.tile(wq, (1, 4))
            base = x @ w.T
            lora = x @ A.T @ B.T
            return base + lora * LORA_SCALING
        key = jax.random.key(seed)
        ks = jax.random.split(key, 10)
        d, h, r = (512, 1376, 2)
        return {'x': jax.random.normal(ks[0], (16, 1, d), dtype=jnp.float32), 'w1q': jax.random.normal(ks[1], (h, d // 4), dtype=jnp.float32) * 0.02, 'a1': jax.random.normal(ks[2], (r, d), dtype=jnp.float32) * 0.02, 'b1': jax.random.normal(ks[3], (h, r), dtype=jnp.float32) * 0.02, 'w3q': jax.random.normal(ks[4], (h, d // 4), dtype=jnp.float32) * 0.02, 'a3': jax.random.normal(ks[5], (r, d), dtype=jnp.float32) * 0.02, 'b3': jax.random.normal(ks[6], (h, r), dtype=jnp.float32) * 0.02, 'w2q': jax.random.normal(ks[7], (d, h // 4), dtype=jnp.float32) * 0.02, 'a2': jax.random.normal(ks[8], (r, h), dtype=jnp.float32) * 0.02, 'b2': jax.random.normal(ks[9], (d, r), dtype=jnp.float32) * 0.02}
    _L0_ffn_in = _L0_ffn_setup()
    _d = {'L0_attn_x': _L0_attn_in['x'], 'L0_attn_Wq_down': _L0_attn_in['Wq_down'], 'L0_attn_Wq_up': _L0_attn_in['Wq_up'], 'L0_attn_Wq_rope': _L0_attn_in['Wq_rope'], 'L0_attn_Wkv_down': _L0_attn_in['Wkv_down'], 'L0_attn_Wk_up': _L0_attn_in['Wk_up'], 'L0_attn_Wv_up': _L0_attn_in['Wv_up'], 'L0_attn_Wk_rope': _L0_attn_in['Wk_rope'], 'L0_attn_Wo': _L0_attn_in['Wo'], 'L0_ffn_w1q': _L0_ffn_in['w1q'], 'L0_ffn_a1': _L0_ffn_in['a1'], 'L0_ffn_b1': _L0_ffn_in['b1'], 'L0_ffn_w3q': _L0_ffn_in['w3q'], 'L0_ffn_a3': _L0_ffn_in['a3'], 'L0_ffn_b3': _L0_ffn_in['b3'], 'L0_ffn_w2q': _L0_ffn_in['w2q'], 'L0_ffn_a2': _L0_ffn_in['a2'], 'L0_ffn_b2': _L0_ffn_in['b2']}
    _x0 = _d['L0_attn_x']
    _d['L0_attn_x'] = jax.random.normal(jax.random.fold_in(jax.random.key(seed), 1), (8, 256, 512), dtype=_x0.dtype)
    del _x0
    return _d

def reference(L0_attn_x, L0_attn_Wq_down, L0_attn_Wq_up, L0_attn_Wq_rope, L0_attn_Wkv_down, L0_attn_Wk_up, L0_attn_Wv_up, L0_attn_Wk_rope, L0_attn_Wo, L0_ffn_w1q, L0_ffn_a1, L0_ffn_b1, L0_ffn_w3q, L0_ffn_a3, L0_ffn_b3, L0_ffn_w2q, L0_ffn_a2, L0_ffn_b2):

    def _L0_attn_ref(x, Wq_down, Wq_up, Wq_rope, Wkv_down, Wk_up, Wv_up, Wk_rope, Wo):
        import jax, jax.numpy as jnp
        import numpy as np
        D_MODEL, N_HEADS, LATENT, ROPE = (512, 128, 64, 64)
        HEAD_DIM = D_MODEL // N_HEADS
        B, S = (2, 128)
        b, s, _ = x.shape
        c_q = x @ Wq_down
        c_kv = x @ Wkv_down
        q_c = (c_q @ Wq_up).reshape(b, s, N_HEADS, HEAD_DIM)
        q_r = (x @ Wq_rope).reshape(b, s, N_HEADS, ROPE)
        k_c = (c_kv @ Wk_up).reshape(b, s, N_HEADS, HEAD_DIM)
        v_c = (c_kv @ Wv_up).reshape(b, s, N_HEADS, HEAD_DIM)
        k_r = x @ Wk_rope
        scale = jnp.asarray((HEAD_DIM + ROPE) ** 0.5, x.dtype)
        scores = (jnp.einsum('bqhd,bkhd->bhqk', q_c, k_c) + jnp.einsum('bqhd,bkd->bhqk', q_r, k_r)) / scale
        attn = jax.nn.softmax(scores, axis=-1)
        out = jnp.einsum('bhqk,bkhd->bqhd', attn, v_c)
        out = out.reshape(b, s, N_HEADS * HEAD_DIM)
        return out @ Wo

    def _L0_ffn_ref(x, w1q, a1, b1, w3q, a3, b3, w2q, a2, b2):
        import jax, jax.numpy as jnp
        import numpy as np
        LORA_SCALING = 1.0 / 2.0

        def _qlora_linear(x, wq, A, B):
            w = jnp.tile(wq, (1, 4))
            base = x @ w.T
            lora = x @ A.T @ B.T
            return base + lora * LORA_SCALING
        gate = jax.nn.silu(_qlora_linear(x, w1q, a1, b1))
        up = _qlora_linear(x, w3q, a3, b3)
        return _qlora_linear(gate * up, w2q, a2, b2)
    x = L0_attn_x
    xn = _layernorm(x, axis=-1)
    s = _L0_attn_ref(xn, L0_attn_Wq_down, L0_attn_Wq_up, L0_attn_Wq_rope, L0_attn_Wkv_down, L0_attn_Wk_up, L0_attn_Wv_up, L0_attn_Wk_rope, L0_attn_Wo)
    g = _silu(_L0_ffn_ref(xn, L0_ffn_w1q, L0_ffn_a1, L0_ffn_b1, L0_ffn_w3q, L0_ffn_a3, L0_ffn_b3, L0_ffn_w2q, L0_ffn_a2, L0_ffn_b2))
    x = x + s * g
    return x

_drawn_inputs = setup_inputs


def setup_inputs(seed=0):
    import zlib

    import numpy as np

    out = dict(_drawn_inputs(seed))
    spreads = {}
    factors = {}
    for name, (base, spread) in spreads.items():
        noise = np.random.default_rng([zlib.crc32(name.encode()), seed]).standard_normal(out[name].shape)
        drawn = base * np.exp(spread * noise) if base else spread * noise
        out[name] = jnp.asarray(drawn.astype(out[name].dtype))
    for name, factor in factors.items():
        out[name] = (out[name] * factor).astype(out[name].dtype)
    return out
```

```python
import concourse.bass as bass
from concourse import mybir
from contextlib import ExitStack

F32 = mybir.dt.float32
F32R = mybir.dt.float32r
ALU = mybir.AluOpType
ACT = mybir.ActivationFunctionType
AX = mybir.AxisListType

B, S, D = 8, 256, 512
T = B * S
H, HD, LAT, ROPE = 128, 4, 64, 64
KD = D // 128
GH = 16
G = H // GH
SH = 4
NS = GH // SH
NT = G * B
SCALE = float(HD + ROPE) ** -0.5
FF = 1376
RANK = 2
FB = FF // 4
FR = [128, 128, FB - 256]
CH = 512
NC = T // CH
EPS = 1e-5


def hold(eng, passed, semaphore, value):
    eng.wait_ge(semaphore, value)
    eng.sem_inc(passed, 1)


def wait(eng, semaphore, value):
    if not (isinstance(value, int) and value <= 0):
        eng.wait_ge(semaphore, value)


def over_chunks(eng, body):
    body(0)
    with eng.Fori(1, NC) as c:
        body(c)


def attn_ffn_layer(nc, x, wq_down, wq_up, wq_rope, wkv_down, wk_up, wv_up, wk_rope, wo,
                   w1qT, a1T, b1T, w3qT, a3T, b3T, w2qT, a2T, b2T, out):
    v_dram = nc.dram_tensor("v_scratch", [T, H * HD], F32, kind="Internal").ap()
    o_dram = nc.dram_tensor("o_scratch", [G, 128, T], F32, kind="Internal").ap()
    x_tok = x.rearrange("b s d -> (b s) d").rearrange("(n p) d -> p n d", p=128)
    out_tok = out.rearrange("b s d -> (b s) d").rearrange("(n p) d -> p n d", p=128)

    top = ExitStack()
    with top:
        def sb(ctx, name, shape, dt=F32):
            return ctx.enter_context(nc.sbuf_tensor(name, shape, dt))

        def sem(name):
            return top.enter_context(nc.semaphore(name))

        xh = sb(top, "xh", [128, KD, T], F32R)
        xl = sb(top, "xl", [128, KD, T], F32R)
        passed = sem("passed")
        attn = ExitStack()
        with attn:
            cT = sb(attn, "cT", [128, T])
            krh = sb(attn, "krh", [128, T], F32R)
            krlh = sb(attn, "krlh", [128, T], F32R)
            w_stage = sb(attn, "w_stage", [128, NS, KD, SH * ROPE])
            wh = sb(attn, "wh", [128, NS, KD, SH * ROPE], F32R)
            wl = sb(attn, "wl", [128, NS, KD, SH * ROPE], F32R)
            up_all = sb(attn, "up_all", [128, G, 128])
            ident = sb(attn, "ident", [128, 128])

            w_staged = [sem(f"w_staged{s}") for s in range(NS)]
            project_inputs(nc, sb, sem, passed, x_tok, wq_down, wkv_down, wk_rope, wv_up, wq_up, wk_up, v_dram,
                           xh, xl, cT, krh, krlh, up_all, ident, w_stage, wq_rope, w_staged)
            attention(nc, sb, sem, passed, xh, xl, cT, krh, krlh, w_stage, wh, wl, wq_rope, w_staged, up_all,
                      ident, v_dram, o_dram)
        finish(nc, sb, sem, passed, x_tok, xh, xl, o_dram, wo, w1qT, a1T, b1T, w3qT, a3T, b3T, w2qT, a2T, b2T,
               out_tok)


def project_inputs(nc, sb, sem, passed, x_tok, wq_down, wkv_down, wk_rope, wv_up, wq_up, wk_up, v_dram,
                   xh, xl, cT, krh, krlh, up_all, ident, w_stage, wq_rope, w_staged):
    NTL = CH // 128
    ctx = ExitStack()
    with ctx:
        x_in = sb(ctx, "x_in", [128, T // 128, D])
        xn = sb(ctx, "xn", [128, NTL, D])
        stats = sb(ctx, "stats", [128, NTL, 6])
        mv = sb(ctx, "mv", [128, NTL, 2])
        var = sb(ctx, "var", [128, NTL])
        std = sb(ctx, "std", [128, NTL])
        rs = sb(ctx, "rs", [128, 4, NTL])
        ws = sb(ctx, "ws", [128, KD, 256])
        wsh = sb(ctx, "wsh", [128, KD, 256], F32R)
        wsl = sb(ctx, "wsl", [128, KD, 256], F32R)
        wv = sb(ctx, "wv", [128, H * HD])
        cc = sb(ctx, "cc", [128, CH])
        vs = sb(ctx, "vs", [128, NTL, H * HD])
        tp = [ctx.enter_context(nc.psum_tensor(f"tp{i}", [128, 512], F32)) for i in range(2)]
        cp = ctx.enter_context(nc.psum_tensor("cp", [128, CH], F32))
        kp = ctx.enter_context(nc.psum_tensor("kp", [128, CH], F32))
        vp = [ctx.enter_context(nc.psum_tensor(f"vp{i}", [128, 512], F32)) for i in range(2)]

        x_loaded = [sem(f"x_loaded{c}") for c in range(NC)]
        small_loaded = sem("small_loaded")
        up_loaded = sem("up_loaded")
        zeroed = sem("zeroed")
        ident_ready = sem("ident_ready")
        ws_hi = sem("ws_hi")
        ws_ready = sem("ws_ready")
        dve_step = sem("dve_step")
        var_ready = sem("var_ready")
        std_ready = sem("std_ready")
        xn_ready = sem("xn_ready")
        transposed = sem("transposed")
        xh_done = sem("xh_done")
        xl_done = sem("xl_done")
        c_done = sem("c_done")
        kr_done = sem("kr_done")
        cc_ready = sem("cc_ready")
        krh_done = sem("krh_done")
        krl_done = sem("krl_done")
        v_done = sem("v_done")
        vs_ready = sem("vs_ready")
        v_stored = sem("v_stored")

        def chunks(eng, body, loaded=None):
            body(0, True)
            if loaded is not None:
                for n in range(1, NC):
                    eng.wait_ge(loaded[n], 16)
            with eng.Fori(1, NC) as c:
                body(c, False)

        block = ctx.enter_context(nc.Block())

        @block.sync
        def _(sp):
            sp.dma_start(x_in[:, 0:NTL, :], x_tok[:, 0:NTL, :]).then_inc(x_loaded[0], 16)
            sp.dma_start(ws[:, :, 0:64], wq_down.rearrange("(k p) n -> p k n", p=128)).then_inc(small_loaded, 16)
            sp.dma_start(ws[:, :, 64:128], wkv_down.rearrange("(k p) n -> p k n", p=128)).then_inc(small_loaded, 16)
            sp.dma_start(ws[:, :, 128:192], wk_rope.rearrange("(k p) n -> p k n", p=128)).then_inc(small_loaded, 16)
            sp.dma_start(ws[:, :, 192:256], wk_rope.rearrange("(k p) n -> p k n", p=128)).then_inc(small_loaded, 16)
            sp.dma_start(wv[64:128, :], wv_up).then_inc(small_loaded, 16)
            for c in range(1, NC):
                sp.dma_start(x_in[:, c * NTL:(c + 1) * NTL, :],
                             x_tok[:, c * NTL:(c + 1) * NTL, :]).then_inc(x_loaded[c], 16)
            sp.wait_ge(zeroed, 2)
            sp.dma_start(up_all[0:64, :, 0:64], wq_up.rearrange("p (g n) -> p g n", g=G)).then_inc(up_loaded, 16)
            sp.dma_start(up_all[64:128, :, 64:128], wk_up.rearrange("p (g n) -> p g n", g=G)).then_inc(up_loaded, 16)
            for s in range(NS):
                sp.dma_start(w_stage[:, s], wq_rope[0, s].rearrange("p (k n) -> p k n", k=KD)).then_inc(w_staged[s], 16)
            def chunk(c):
                hold(sp, passed, vs_ready, (c + 1) * NTL)
                sp.dma_start(v_dram[bass.ds(c * CH, CH), :].rearrange("(n p) d -> p n d", p=128),
                             vs[:, :, :]).then_inc(v_stored, 16)

            over_chunks(sp, chunk)
            sp.wait_ge(v_stored, 16 * NC)
            sp.wait_ge(up_loaded, 32)

        @block.gpsimd
        def _(pool):
            nc.gpsimd.memset(ident[:, :], 0.0).then_inc(zeroed, 1)
            nc.gpsimd.memset(up_all[:, :, :], 0.0).then_inc(zeroed, 1)
            pool.wait_ge(zeroed, 2)
            nc.gpsimd.affine_select(out=ident[:, :], in_=ident[:, :], compare_op=ALU.not_equal, fill=1.0,
                                    base=0, pattern=[[-1, 128]], channel_multiplier=1).then_inc(ident_ready, 1)
            pool.wait_ge(ident_ready, 1)
            def chunk(c):
                hold(pool, passed, krh_done, c + 1)
                nc.gpsimd.tensor_copy(krlh[64:128, bass.ds(c * CH, CH)],
                                      krh[64:128, bass.ds(c * CH, CH)]).then_inc(krl_done, 1)

            over_chunks(pool, chunk)

        @block.scalar
        def _(act):
            act.wait_ge(small_loaded, 80)
            nc.scalar.activation(wsh[:, :, :], ws[:, :, :], ACT.Copy).then_inc(ws_hi, 1)
            def body(c, first):
                act.wait_ge(var_ready, c + 1)
                nc.scalar.activation(std[:, :], var[:, :], ACT.Sqrt).then_inc(std_ready, 1)
                for i in range(NTL):
                    act.wait_ge(transposed, c * NTL + i + 1)
                    nc.scalar.activation(xh[:, :, bass.ds(c * CH + i * 128, 128)],
                                         tp[i % 2][:, :].rearrange("p (k n) -> p k n", k=KD),
                                         ACT.Copy).then_inc(xh_done, 1)
                act.wait_ge(c_done, c + 1)
                wait(act, v_done, c * NTL)
                nc.scalar.activation(cc[:, :], cp[:, :], ACT.Copy).then_inc(cc_ready, 1)
                act.wait_ge(kr_done, c + 1)
                nc.scalar.activation(krh[:, bass.ds(c * CH, CH)], kp[:, :], ACT.Copy).then_inc(krh_done, 1)
                act.wait_ge(cc_ready, c + 1)
                nc.scalar.activation(cT[:, bass.ds(c * CH, CH)], cc[:, :], ACT.Copy)
                for i in range(NTL):
                    act.wait_ge(v_done, c * NTL + i + 1)
                    if i == 0:
                        wait(act, v_stored, 16 * c)
                    nc.scalar.activation(vs[:, i, :], vp[i % 2][:, :], ACT.Copy).then_inc(vs_ready, 1)

            chunks(act, body)

        @block.vector
        def _(dve):
            def body(c, first):
                steps = [0]

                def link(ins):
                    steps[0] += 1
                    ins.then_inc(dve_step, 1)
                    hold(dve, passed, dve_step, c * 7 + steps[0])

                for i in range(NTL):
                    last = nc.vector.bn_stats(stats[:, i, :], x_in[:, bass.ds(c * NTL + i, 1), :].rearrange("p a d -> p (a d)"))
                link(last)
                for i in range(NTL):
                    last = nc.vector.bn_aggr(mv[:, i, :], stats[:, i, :])
                link(last)
                nc.vector.tensor_scalar(var[:, :], mv[:, :, 1], EPS, None, ALU.add).then_inc(var_ready, 1)
                dve.wait_ge(std_ready, c + 1)
                link(nc.vector.reciprocal(rs[:, 0, :], std[:, :]))
                link(nc.vector.tensor_tensor(rs[:, 1, :], rs[:, 0, :], rs[:, 0, :], ALU.mult))
                link(nc.vector.tensor_tensor(rs[:, 2, :], rs[:, 1, :], var[:, :], ALU.mult))
                link(nc.vector.tensor_scalar(rs[:, 1, :], rs[:, 2, :], -0.5, 1.5, ALU.mult, ALU.add))
                link(nc.vector.tensor_tensor(rs[:, 3, :], rs[:, 1, :], rs[:, 0, :], ALU.mult))
                wait(dve, transposed, c * NTL)
                for i in range(NTL):
                    nc.vector.tensor_scalar(xn[:, i, :], x_in[:, bass.ds(c * NTL + i, 1), :].rearrange("p a d -> p (a d)"),
                                            mv[:, i, 0:1], rs[:, 3, i:i + 1], ALU.subtract, ALU.mult).then_inc(xn_ready, 1)
                for i in range(NTL):
                    dve.wait_ge(xh_done, c * NTL + i + 1)
                    xs = bass.ds(c * CH + i * 128, 128)
                    nc.vector.tensor_tensor(xl[:, :, xs], tp[i % 2][:, :].rearrange("p (k n) -> p k n", k=KD),
                                            xh[:, :, xs], ALU.subtract).then_inc(xl_done, 1)
                if first:
                    dve.wait_ge(ws_hi, 1)
                    nc.vector.tensor_tensor(wsl[:, :, :], ws[:, :, :], wsh[:, :, :], ALU.subtract).then_inc(ws_ready, 1)
                dve.wait_ge(krh_done, c + 1)
                nc.vector.tensor_tensor(krlh[0:64, bass.ds(c * CH, CH)], kp[0:64, :],
                                        krh[0:64, bass.ds(c * CH, CH)], ALU.subtract).then_inc(krl_done, 1)

            dve.wait_ge(x_loaded[0], 16)
            chunks(dve, body, x_loaded)

        @block.tensor
        def _(pe):
            pe.wait_ge(ident_ready, 1)
            pe.wait_ge(small_loaded, 80)
            def chunk(c):
                for i in range(NTL):
                    pe.wait_ge(xn_ready, c * NTL + i + 1)
                    if i < 2:
                        wait(pe, xl_done, c * NTL)
                    else:
                        pe.wait_ge(xl_done, c * NTL + i - 1)
                    for k in range(KD):
                        last = nc.tensor.transpose(tp[i % 2][:, k * 128:(k + 1) * 128],
                                                   xn[:, i, k * 128:(k + 1) * 128], ident[:, :])
                    last.then_inc(transposed, 1)
                pe.wait_ge(xl_done, (c + 1) * NTL)
                pe.wait_ge(ws_ready, 1)
                xs = bass.ds(c * CH, CH)
                wait(pe, cc_ready, c)
                for dst, lo, done in ((cp, 0, c_done), (kp, 128, kr_done)):
                    if lo:
                        wait(pe, krl_done, 2 * c)
                    for k in range(KD):
                        for n, (w, xx) in enumerate(((wsh, xh), (wsh, xl), (wsl, xh))):
                            last = nc.tensor.matmul(dst[:, :], w[:, k, lo:lo + 128], xx[:, k, xs],
                                                    start=(k == 0 and n == 0), stop=(k == KD - 1 and n == 2))
                    last.then_inc(done, 1)
                pe.wait_ge(cc_ready, c + 1)
                for i in range(NTL):
                    if i < 2:
                        wait(pe, vs_ready, c * NTL)
                    else:
                        pe.wait_ge(vs_ready, c * NTL + i - 1)
                    nc.tensor.matmul(vp[i % 2][:, :], cc[64:128, i * 128:(i + 1) * 128], wv[64:128, :],
                                     start=True, stop=True).then_inc(v_done, 1)

            over_chunks(pe, chunk)


def attention(nc, sb, sem, passed, xh, xl, cT, krh, krlh, w_stage, wh, wl, wq_rope, w_staged, up_all, ident,
              v_dram, o_dram):
    KC = 64 + 3 * HD * SH
    ctx = ExitStack()
    with ctx:
        slot1 = sb(ctx, "slot1", [128, NS, SH, S], F32R)
        slot2 = sb(ctx, "slot2", [128, NS, SH, S], F32R)
        k1 = sb(ctx, "k1", [128, NS, S], F32R)
        k2 = sb(ctx, "k2", [128, NS, S], F32R)
        content = sb(ctx, "content", [128, 3, S], F32R)
        up = sb(ctx, "up", [128, 128])
        probs = sb(ctx, "probs", [128, 2, SH, S])
        v_it = sb(ctx, "v_it", [128, 2, 2, GH * HD])
        vx = sb(ctx, "vx", [128, NS, 2, SH, 32])
        mx = sb(ctx, "mx", [128, NS, SH * 2])
        mrow = sb(ctx, "mrow", [SH * 2, NS, 128], F32R)
        o_sb = sb(ctx, "o_sb", [128, S])

        st = ctx.enter_context(nc.psum_tensor("st", [128, 2, SH, S], F32))
        sx = ctx.enter_context(nc.psum_tensor("sx", [128, 2, 512], F32))
        pj = ctx.enter_context(nc.psum_tensor("pj", [128, 2, S], F32))
        ob = ctx.enter_context(nc.psum_tensor("ob", [128, 2, S], F32))

        init_done = sem("init_done")
        w_hi = sem("w_hi")
        w_ready = sem("w_ready")
        up_ready = sem("up_ready")
        proj_done = sem("proj_done")
        qh_done = sem("qh_done")
        ql_done = sem("ql_done")
        s2_done = sem("s2_done")
        k_ready = sem("k_ready")
        content_done = sem("content_done")
        ct_hi = sem("ct_hi")
        ct_lo = sem("ct_lo")
        ct_copy = sem("ct_copy")
        ct_in = [sem(f"ct_in{s}") for s in range(NS)]
        smax_done = sem("smax_done")
        max_done = sem("max_done")
        mt_done = sem("mt_done")
        mrow_ready = sem("mrow_ready")
        mrow_in = [sem(f"mrow_in{s}") for s in range(NS)]
        st_done = sem("st_done")
        exp_done = sem("exp_done")
        v_loaded = sem("v_loaded")
        vx_ready = sem("vx_ready")
        av_done = sem("av_done")
        o_evac = sem("o_evac")
        o_stored = sem("o_stored")

        def iterations(eng, body):
            body(0, True, False, True)
            with eng.Fori(1, NT - 1) as t:
                body(t, False, False, True)
            body(NT - 1, False, False, False)
            body(NT, False, True, False)

        block = ctx.enter_context(nc.Block())

        @block.sync
        def _(sp):
            def load_content(tt, s):
                hold(sp, passed, ct_hi, tt + 1)
                hold(sp, passed, ct_lo, 2 * (tt + 1))
                hold(sp, passed, ct_copy, tt + 1)
                sp.dma_start(k1[64:KC, s, :].bitcast(F32),
                             content[64 + 16 * s:80 + 16 * s, :, :].bitcast(F32)).then_inc(ct_in[s], 16)
                for j in range(SH):
                    r = 64 + 12 * j
                    sp.dma_start(slot1[r:r + 12, s, j, :].bitcast(F32),
                                 content[16 * s + 4 * j:16 * s + 4 * j + 4, :, :].bitcast(F32)).then_inc(ct_in[s], 16)

            def load_v(tt, par):
                g, b = tt // B, tt % B
                sp.dma_start(v_it[:, bass.ds(par, 1), :, :].rearrange("p a k n -> p (a k) n"),
                             v_dram[bass.ds(b * S, S), bass.ds(g * (GH * HD), GH * HD)]
                             .rearrange("(k p) n -> p k n", p=128)).then_inc(v_loaded, 16)

            def store_o(tt):
                hold(sp, passed, o_evac, tt + 1)
                sp.dma_start(o_dram[bass.ds(tt // B, 1), :, bass.ds((tt % B) * S, S)]
                             .rearrange("a p n -> (a p) n"), o_sb[:, :]).then_inc(o_stored, 16)

            def max_row(tt, s, v):
                hold(sp, passed, mrow_ready, v + 1)
                sp.dma_start(slot1[112:113, s, :, :].bitcast(F32),
                             mrow[:, s, :].bitcast(F32)).then_inc(mrow_in[s], 16)

            def body(t, first, stage):
                for s in range(NS):
                    u = t * NS + s
                    if not first or s >= 2:
                        max_row(t, (s + 2) % NS, u - 2)
                    if not first or s >= 3:
                        hold(sp, passed, st_done, u * 2 - 4)
                    if s < NS - 1:
                        load_content(t, s + 1)
                    else:
                        load_content(t + 1, 0)
                        hold(sp, passed, vx_ready, t * NS + 1)
                        load_v(t + 1, (t + 1) % 2)
                        if not first:
                            store_o(t - 1)
                    if stage is not None:
                        hold(sp, passed, w_ready, stage * NS + s + 1)
                        sp.dma_start(w_stage[:, s], wq_rope[bass.ds(stage + 1, 1), s].rearrange("a p (k n) -> (a p) k n", k=KD)).then_inc(w_staged[s], 16)

            sp.sem_inc(o_stored, 16)
            sp.wait_ge(init_done, 3)
            load_v(0, 0)
            load_content(0, 0)
            body(0, True, 0)
            with sp.Fori(1, B) as b:
                body(b, False, None)
            with sp.Fori(1, G - 1) as g:
                body(g * B, False, g)
                with sp.Fori(1, B) as b:
                    body(g * B + b, False, None)
            with sp.Fori((G - 1) * B, NT - 1) as t:
                body(t, False, None)
            t = NT - 1
            for s in range(NS):
                u = t * NS + s
                max_row(t, (s + 2) % NS, u - 2)
                if s < NS - 1:
                    hold(sp, passed, st_done, u * 2 - 4)
                    load_content(t, s + 1)
                else:
                    store_o(t - 1)
            for s in range(2):
                max_row(NT, (s + 2) % NS, NT * NS + s - 2)
            store_o(NT - 1)
            sp.wait_ge(o_stored, 16 * (NT + 1))

        @block.gpsimd
        def _(pool):
            nc.gpsimd.memset(slot1[:, :, :, :].bitcast(F32), 0.0).then_inc(init_done, 1)
            nc.gpsimd.memset(k1[:, :, :].bitcast(F32), -1.0).then_inc(init_done, 1)
            nc.gpsimd.memset(vx[:, :, :, :, :], 0.0).then_inc(init_done, 1)
            pool.wait_ge(init_done, 3)
            for s in range(NS):
                nc.gpsimd.memset(vx[:, s, :, :, 16 + 4 * s:20 + 4 * s], 1.0).then_inc(init_done, 1)

            def refill(g, s):
                hold(pool, passed, w_staged[s], 16 * (g + 1))
                nc.gpsimd.tensor_copy(wh[:, s], w_stage[:, s]).then_inc(w_hi, 1)
                hold(pool, passed, w_hi, g * NS + s + 1)
                nc.gpsimd.tensor_tensor(wl[:, s], w_stage[:, s], wh[:, s], ALU.subtract).then_inc(w_ready, 1)

            def copy_up(g):
                nc.gpsimd.tensor_copy(up[:, :], up_all[:, bass.ds(g, 1), :].rearrange("p a n -> p (a n)")).then_inc(up_ready, 1)

            def body(t, b, first, refill_g):
                if refill_g is not None:
                    hold(pool, passed, content_done, t + 1)
                    copy_up(refill_g)
                bs = bass.ds(b * S, S)
                for s in range(NS):
                    u = t * NS + s
                    if not first:
                        hold(pool, passed, st_done, u * 2 - 6)
                    nc.gpsimd.tensor_copy(k1[0:64, s, :], krh[0:64, bs]).then_inc(k_ready, 1)
                    nc.gpsimd.tensor_copy(k2[:, s, :], krlh[:, bs]).then_inc(k_ready, 1)
                    if not first:
                        hold(pool, passed, av_done, u - 3)
                    if s == 0:
                        hold(pool, passed, v_loaded, 16 * (t + 1))
                    nc.gpsimd.tensor_copy(
                        vx[:, s, :, :, 4 * s:4 * s + 4],
                        v_it[:, bass.ds(t % 2, 1)].rearrange("p a k (j r) -> p (a k) j r", j=SH)
                        [:, :, :, 4 * s:4 * s + 4]).then_inc(vx_ready, 1)
                    if s == NS - 1:
                        content_copies(t + 1)
                    if refill_g is not None:
                        hold(pool, passed, qh_done, 2 * u + 2)
                        refill(refill_g, s)

            def content_copies(tt):
                hold(pool, passed, ct_hi, tt + 1)
                nc.gpsimd.tensor_copy(content[0:64, 2, :], content[0:64, 0, :]).then_inc(ct_copy, 1)

            copy_up(0)
            for s in range(NS):
                refill(0, s)
            content_copies(0)
            body(0, 0, True, None)
            with pool.Fori(1, B - 1) as b:
                body(b, b, False, None)
            body(B - 1, B - 1, False, 1)
            with pool.Fori(1, G - 1) as g:
                with pool.Fori(0, B - 1) as b:
                    body(g * B + b, b, False, None)
                body(g * B + (B - 1), B - 1, False, g + 1)
            with pool.Fori(0, B - 1) as b:
                body(b + (G - 1) * B, b, False, None)
            t = NT - 1
            for s in range(NS):
                u = t * NS + s
                hold(pool, passed, st_done, u * 2 - 6)
                nc.gpsimd.tensor_copy(k1[0:64, s, :], krh[0:64, (B - 1) * S:B * S]).then_inc(k_ready, 1)
                nc.gpsimd.tensor_copy(k2[:, s, :], krlh[:, (B - 1) * S:B * S]).then_inc(k_ready, 1)
                hold(pool, passed, av_done, u - 3)
                if s == 0:
                    hold(pool, passed, v_loaded, 16 * (t + 1))
                nc.gpsimd.tensor_copy(
                    vx[:, s, :, :, 4 * s:4 * s + 4],
                    v_it[:, t % 2].rearrange("p k (j r) -> p k j r", j=SH)[:, :, :, 4 * s:4 * s + 4]).then_inc(vx_ready, 1)

        @block.scalar
        def _(act):
            def content_hi(tt):
                act.wait_ge(content_done, tt + 1)
                nc.scalar.activation(content[64:128, 1, :], ob[64:128, 1, :], ACT.Copy)
                nc.scalar.activation(content[:, 0, :], ob[:, 1, :], ACT.Copy).then_inc(ct_hi, 1)

            def body(t, first, last, more):
                for s in range(NS if not last else 3):
                    u = t * NS + s
                    has_v = not first or s >= 3
                    if s == NS - 1 and not first:
                        act.wait_ge(av_done, t * NS)
                        act.wait_ge(o_stored, 16 * t)
                        nc.scalar.activation(o_sb[:, :], ob[:, 0, :], ACT.Copy).then_inc(o_evac, 1)
                    for kt in range(2):
                        if has_v:
                            v = u - 3
                            act.wait_ge(st_done, 2 * v + kt + 1)
                            if kt == 0 and not (first and s == 3):
                                act.wait_ge(av_done, v)
                            nc.scalar.activation(probs[:, kt], st[:, kt], ACT.Exp, scale=SCALE).then_inc(exp_done, 1)
                        if s == NS - 1 and kt == 0 and more:
                            for n in range(NS):
                                act.wait_ge(ct_in[n], 80 * (t + 1))
                            content_hi(t + 1)
                    if not last:
                        act.wait_ge(proj_done, u + 1)
                        if not first:
                            act.wait_ge(st_done, u * 2 - 6)
                        for e in range(2):
                            nc.scalar.activation(slot1[0:64, s, e:SH:2, :], pj[64 * e:64 * e + 64, :, :],
                                                 ACT.Copy).then_inc(qh_done, 1)

            act.wait_ge(init_done, 3)
            content_hi(0)
            iterations(act, body)
            act.wait_ge(av_done, NT * NS)
            act.wait_ge(o_stored, 16 * NT)
            nc.scalar.activation(o_sb[:, :], ob[:, 0, :], ACT.Copy).then_inc(o_evac, 1)

        @block.vector
        def _(dve):
            def content_lo(tt):
                dve.wait_ge(ct_hi, tt + 1)
                for lo, piece in ((0, 1), (64, 2)):
                    nc.vector.tensor_tensor(content[lo:lo + 64, piece, :], ob[lo:lo + 64, 1, :],
                                            content[lo:lo + 64, 0, :], ALU.subtract).then_inc(ct_lo, 1)

            def body(t, first, last, more):
                for s in range(NS if not last else 2):
                    u = t * NS + s
                    if not first or s >= 2:
                        sv = (s + 2) % NS
                        dve.wait_ge(mt_done, u - 1)
                        nc.vector.tensor_copy(mrow[:, sv, :], sx[0:SH * 2, 0, 0:128]).then_inc(mrow_ready, 1)
                    if (not first or s >= 1) and not (last and s >= 1):
                        dve.wait_ge(qh_done, 2 * u)
                        sv = (s + 3) % NS
                        nc.vector.tensor_copy(slot2[0:64, sv, :, :], slot1[0:64, sv, :, :]).then_inc(s2_done, 1)
                    if (not first or s >= 1) and not (last and s >= 1):
                        v, sv = u - 1, (s + 3) % NS
                        for j in range(SH):
                            if j == 2 and s == NS - 1 and more:
                                content_lo(t + 1)
                            dve.wait_ge(smax_done, v * SH + j + 1)
                            nc.vector.tensor_reduce(mx[:, sv, 2 * j:2 * j + 2],
                                                    sx[:, j % 2, :].rearrange("p (a k) -> p a k", a=2),
                                                    axis=AX.X, op=ALU.max).then_inc(max_done, 1)
                    if not last:
                        for e in range(2):
                            dve.wait_ge(qh_done, 2 * u + e + 1)
                            nc.vector.tensor_tensor(slot2[64:128, s, e:SH:2, :], pj[64 * e:64 * e + 64, :, :],
                                                    slot1[0:64, s, e:SH:2, :], ALU.subtract).then_inc(ql_done, 1)

            content_lo(0)
            iterations(dve, body)

        @block.tensor
        def _(pe):
            def content_product(tt):
                pe.wait_ge(up_ready, tt // B + 1)
                nc.tensor.matmul(ob[:, 1, :], up[:, :], cT[:, bass.ds((tt % B) * S, S)],
                                 start=True, stop=True).then_inc(content_done, 1)

            def transpose_max(s, v):
                pe.wait_ge(max_done, v * SH + SH)
                nc.tensor.transpose(sx[0:SH * 2, 0, 0:128], mx[:, s, :], ident[:, :]).then_inc(mt_done, 1)

            def scores(s, v, first, between=None):
                pe.wait_ge(ql_done, 2 * v + 2)
                pe.wait_ge(s2_done, v + 1)
                for kt in range(2):
                    ks = slice(kt * 128, kt * 128 + 128)
                    if not first:
                        pe.wait_ge(exp_done, 2 * v - 1 + kt)
                    for n, (kk, q, rows) in enumerate(((k1, slot1, KC + 1), (k2, slot2, 128))):
                        for hf in range(2):
                            last = nc.tensor.matmul(st[:, kt, 2 * hf:2 * hf + 2, :], kk[0:rows, s, ks],
                                                    q[0:rows, s, 2 * hf:2 * hf + 2, :],
                                                    start=(n == 0), stop=(n == 1))
                    last.then_inc(st_done, 1)
                    if kt == 0 and between is not None:
                        transpose_max(*between)

            def row_scores(s, v, j, first):
                if j >= 2 or not first:
                    pe.wait_ge(max_done, v * SH + j - 1)
                for qt in range(2):
                    last = nc.tensor.matmul(sx[:, j % 2, qt * S:(qt + 1) * S],
                                            slot1[0:KC, s, j, qt * 128:qt * 128 + 128], k1[0:KC, s, :],
                                            start=True, stop=True)
                last.then_inc(smax_done, 1)

            def project(t, s, bs):
                for p in range(2):
                    for k in range(KD):
                        for n, (w, xx) in enumerate(((wh, xh), (wh, xl), (wl, xh))):
                            last = nc.tensor.matmul(pj[:, p, :], w[:, s, k, 128 * p:128 * p + 128], xx[:, k, bs],
                                                    start=(k == 0 and n == 0), stop=(k == KD - 1 and n == 2))
                last.then_inc(proj_done, 1)

            def values(s, v):
                for kt in range(2):
                    for j in range(SH):
                        last = nc.tensor.matmul(ob[32 * j:32 * j + 32, 0, :], vx[:, s, kt, j, :], probs[:, kt, j, :],
                                                start=(s == 0 and kt == 0), stop=(s == NS - 1 and kt == 1),
                                                tile_position=(0, 32 * j))
                last.then_inc(av_done, 1)

            def body(t, first, last, more):
                bs = bass.ds((t % B) * S, S)
                for s in range(NS if not last else 3):
                    u = t * NS + s
                    has_v3 = not first or s >= 3
                    has_v1 = (not first or s >= 1) and not (last and s >= 1)
                    s3, s1 = (s + 1) % NS, (s + 3) % NS
                    if has_v3:
                        v = u - 3
                        tv = t if s == 3 else t - 1
                        pe.wait_ge(mrow_in[s3], 16 * (tv + 1))
                        scores(s3, v, first, ((s + 2) % NS, u - 2) if not last or s < 2 else None)
                    elif first and s == 2:
                        transpose_max(0, 0)
                    if s == NS - 1:
                        if not first:
                            pe.wait_ge(o_evac, t)
                        if more:
                            content_product(t + 1)
                    if has_v1:
                        v = u - 1
                        tv = t if s >= 1 else t - 1
                        pe.wait_ge(qh_done, 2 * v + 2)
                        pe.wait_ge(ct_in[s1], 80 * (tv + 1))
                        pe.wait_ge(k_ready, 2 * v + 2)
                        if not (first and s == 1):
                            pe.wait_ge(mrow_ready, v)
                        row_scores(s1, v, 0, first and s == 1)
                        row_scores(s1, v, 1, first and s == 1)
                    if not last:
                        pe.wait_ge(w_ready, (t // B) * NS + s + 1)
                        if not (first and s == 0):
                            pe.wait_ge(ql_done, 2 * u)
                        project(t, s, bs)
                    if has_v1:
                        row_scores(s1, u - 1, 2, False)
                        row_scores(s1, u - 1, 3, False)
                    if has_v3:
                        v = u - 3
                        pe.wait_ge(exp_done, 2 * v + 2)
                        pe.wait_ge(vx_ready, v + 1)
                        if s == NS - 1 and more:
                            pe.wait_ge(ct_lo, 2 * (t + 2))
                        values(s3, v)

            pe.wait_ge(init_done, 7)
            content_product(0)
            pe.wait_ge(ct_lo, 2)
            iterations(pe, body)


def finish(nc, sb, sem, passed, x_tok, xh, xl, o_dram, wo, w1qT, a1T, b1T, w3qT, a3T, b3T, w2qT, a2T, b2T, out_tok):
    ctx = ExitStack()
    with ctx:
        NR = len(FR)
        w13h = sb(ctx, "w13h", [128, 2, FF], F32R)
        w13l = sb(ctx, "w13l", [128, 2, FF], F32R)
        w2h = sb(ctx, "w2h", [128, NR, D], F32R)
        w2l = sb(ctx, "w2l", [128, NR, D], F32R)
        woh = sb(ctx, "woh", [128, KD, D], F32R)
        wol = sb(ctx, "wol", [128, KD, D], F32R)
        b13 = sb(ctx, "b13", [96, 2, FF], F32R)
        lr = sb(ctx, "lr", [96, T], F32R)
        sh = sb(ctx, "sh", [128, T], F32R)
        sl = sb(ctx, "sl", [128, T], F32R)
        a2 = sb(ctx, "a2", [128, NR, 4, 32])
        b2 = sb(ctx, "b2", [128, D])

        setup_ffn(nc, sb, sem, passed, xh, xl, wo, w1qT, a1T, b1T, w3qT, a3T, b3T, w2qT, a2T, b2T,
                  w13h, w13l, w2h, w2l, woh, wol, b13, lr, sh, sl, a2, b2)
        ffn_and_output(nc, sb, sem, passed, x_tok, xh, xl, o_dram, w13h, w13l, w2h, w2l, woh, wol, b13, lr, sh, sl,
                       a2, b2, out_tok)


def setup_ffn(nc, sb, sem, passed, xh, xl, wo, w1qT, a1T, b1T, w3qT, a3T, b3T, w2qT, a2T, b2T,
              w13h, w13l, w2h, w2l, woh, wol, b13, lr, sh, sl, a2, b2):
    NR = len(FR)
    ctx = ExitStack()
    with ctx:
        raw13 = sb(ctx, "raw13", [128, 2, FF])
        raw2 = sb(ctx, "raw2", [128, NR, D])
        rawo = sb(ctx, "rawo", [128, KD, D])
        rawa = sb(ctx, "rawa", [128, KD, 2 * RANK])
        la = sb(ctx, "la", [128, KD, 128])
        lah = sb(ctx, "lah", [128, KD, 128], F32R)
        lal = sb(ctx, "lal", [128, KD, 128], F32R)
        one = sb(ctx, "one", [128, 128])
        oner = sb(ctx, "oner", [128, 128], F32R)
        lrt = sb(ctx, "lrt", [96, CH], F32R)
        sp_ = ctx.enter_context(nc.psum_tensor("sump", [128, CH], F32))
        lp = ctx.enter_context(nc.psum_tensor("lp", [128, CH], F32))

        loaded = [sem(f"fl{i}") for i in range(5)]
        zeroed = sem("f_zeroed")
        pads = sem("f_pads")
        eye = sem("f_eye")
        la_ready = sem("f_la_ready")
        la_hi = sem("f_la_hi")
        la_split = sem("f_la_split")
        hi = sem("f_hi")
        lo = sem("f_lo")
        sum_done = sem("f_sum_done")
        lp_done = sem("f_lp_done")
        sh_done = sem("f_sh_done")
        sl_done = sem("f_sl_done")
        lrh_done = sem("f_lrh_done")
        lr_done = sem("f_lr_done")
        b_hi = sem("f_b_hi")
        block = ctx.enter_context(nc.Block())

        @block.sync
        def _(sp):
            sp.dma_start(rawa[:, :, 0:RANK], a1T.rearrange("(k p) n -> p k n", p=128)).then_inc(loaded[0], 16)
            sp.dma_start(rawa[:, :, RANK:2 * RANK], a3T.rearrange("(k p) n -> p k n", p=128)).then_inc(loaded[0], 16)
            sp.dma_start(raw13[:, 0, :], w1qT).then_inc(loaded[1], 16)
            sp.dma_start(raw13[:, 1, :], w3qT).then_inc(loaded[1], 16)
            sp.dma_start(raw2[:, 0:2, :], w2qT[0:256, :].rearrange("(k p) n -> p k n", p=128)).then_inc(loaded[2], 16)
            sp.dma_start(raw2[0:FR[2], 2, :], w2qT[256:FB, :]).then_inc(loaded[2], 16)
            sp.dma_start(rawo[:, :, :], wo.rearrange("(k p) n -> p k n", p=128)).then_inc(loaded[2], 16)
            sp.wait_ge(zeroed, 4)
            for r in range(NR):
                sp.dma_start(a2[0:FR[r], r, :, 0:RANK],
                             a2T.rearrange("(j p) n -> p j n", j=4)[128 * r:128 * r + FR[r], :, :]).then_inc(pads, 16)
            for j in range(4):
                sp.dma_start(b2[32 * j:32 * j + RANK, :], b2T).then_inc(pads, 16)
            sp.wait_ge(hi, 1)
            sp.wait_ge(lo, 1)
            sp.wait_ge(b_hi, 1)
            for r in (0, 32, 64):
                sp.dma_start(raw13[r:r + RANK, 0, :], b1T).then_inc(loaded[4], 16)
                sp.dma_start(raw13[r + RANK:r + 2 * RANK, 1, :], b3T).then_inc(loaded[4], 16)
            sp.wait_ge(pads, 16 * 7)

        @block.gpsimd
        def _(pool):
            nc.gpsimd.memset(one[:, :], 0.0).then_inc(zeroed, 1)
            nc.gpsimd.memset(la[:, :, :], 0.0).then_inc(zeroed, 1)
            nc.gpsimd.memset(a2[:, :, :, :], 0.0).then_inc(zeroed, 1)
            nc.gpsimd.memset(b2[:, :], 0.0).then_inc(zeroed, 1)
            pool.wait_ge(zeroed, 4)
            nc.gpsimd.affine_select(out=one[:, :], in_=one[:, :], compare_op=ALU.not_equal, fill=1.0,
                                    base=0, pattern=[[-1, 128]], channel_multiplier=1).then_inc(eye, 1)
            pool.wait_ge(loaded[0], 32)
            for c in (0, 32, 64):
                nc.gpsimd.tensor_copy(la[:, :, c:c + 2 * RANK], rawa[:, :, :]).then_inc(la_ready, 1)
            pool.wait_ge(hi, 1)
            pool.wait_ge(lo, 1)
            nc.gpsimd.memset(raw13[0:96, :, :], 0.0).then_inc(b_hi, 1)

        @block.scalar
        def _(act):
            act.wait_ge(eye, 1)
            nc.scalar.activation(oner[:, :], one[:, :], ACT.Copy).then_inc(la_hi, 1)
            act.wait_ge(la_ready, 3)
            nc.scalar.activation(lah[:, :, :], la[:, :, :], ACT.Copy).then_inc(la_hi, 1)
            act.wait_ge(loaded[1], 32)
            nc.scalar.activation(w13h[:, :, :], raw13[:, :, :], ACT.Copy).then_inc(hi, 1)
            def chunk(c):
                cs = bass.ds(c * CH, CH)
                act.wait_ge(sum_done, c + 1)
                nc.scalar.activation(sh[:, cs], sp_[:, :], ACT.Copy).then_inc(sh_done, 1)
                act.wait_ge(lp_done, c + 1)
                wait(act, lr_done, c)
                nc.scalar.activation(lr[0:64, cs], lp[0:64, :], ACT.Copy, scale=0.5)
                nc.scalar.activation(lrt[64:96, :], lp[64:96, :], ACT.Copy, scale=0.5).then_inc(lrh_done, 1)

            over_chunks(act, chunk)
            act.wait_ge(loaded[2], 48)
            nc.scalar.activation(w2h[:, 0:2, :], raw2[:, 0:2, :], ACT.Copy)
            nc.scalar.activation(w2h[0:FR[2], 2, :], raw2[0:FR[2], 2, :], ACT.Copy)
            nc.scalar.activation(woh[:, :, :], rawo[:, :, :], ACT.Copy).then_inc(hi, 1)
            act.wait_ge(loaded[4], 96)
            nc.scalar.activation(b13[0:32, :, :], raw13[0:32, :, :], ACT.Copy)
            nc.scalar.activation(b13[64:96, :, :], raw13[64:96, :, :], ACT.Copy)
            nc.scalar.activation(b13[32:64, :, :], raw13[32:64, :, :], ACT.Copy).then_inc(hi, 1)

        @block.vector
        def _(dve):
            dve.wait_ge(la_hi, 2)
            nc.vector.tensor_tensor(lal[:, :, :], la[:, :, :], lah[:, :, :], ALU.subtract).then_inc(la_split, 1)
            dve.wait_ge(hi, 1)
            nc.vector.tensor_tensor(w13l[:, :, :], raw13[:, :, :], w13h[:, :, :], ALU.subtract).then_inc(lo, 1)
            def chunk(c):
                cs = bass.ds(c * CH, CH)
                dve.wait_ge(sh_done, c + 1)
                nc.vector.tensor_tensor(sl[:, cs], sp_[:, :], sh[:, cs], ALU.subtract).then_inc(sl_done, 1)
                dve.wait_ge(lrh_done, c + 1)
                nc.vector.scalar_tensor_tensor(out=lr[64:96, cs], in0=lp[64:96, :], scalar=0.5, in1=lrt[64:96, :],
                                               op0=ALU.mult, op1=ALU.subtract).then_inc(lr_done, 1)

            over_chunks(dve, chunk)
            dve.wait_ge(hi, 2)
            nc.vector.tensor_tensor(w2l[:, 0:2, :], raw2[:, 0:2, :], w2h[:, 0:2, :], ALU.subtract)
            nc.vector.tensor_tensor(w2l[0:FR[2], 2, :], raw2[0:FR[2], 2, :], w2h[0:FR[2], 2, :], ALU.subtract)
            nc.vector.tensor_tensor(wol[:, :, :], rawo[:, :, :], woh[:, :, :], ALU.subtract).then_inc(lo, 1)
            dve.wait_ge(hi, 3)
            nc.vector.tensor_tensor(b13[32:64, :, :], raw13[32:64, :, :], b13[32:64, :, :], ALU.subtract).then_inc(lo, 1)

        @block.tensor
        def _(pe):
            pe.wait_ge(la_hi, 2)
            pe.wait_ge(la_split, 1)
            def chunk(c):
                cs = bass.ds(c * CH, CH)
                wait(pe, sl_done, c)
                for k in range(KD):
                    for xx in (xh, xl):
                        last = nc.tensor.matmul(sp_[:, :], oner[:, :], xx[:, k, cs],
                                                start=(k == 0 and xx is xh), stop=(k == KD - 1 and xx is xl))
                last.then_inc(sum_done, 1)
                wait(pe, lr_done, c)
                for k in range(KD):
                    for n, (w, xx) in enumerate(((lah, xh), (lah, xl), (lal, xh))):
                        last = nc.tensor.matmul(lp[:, :], w[:, k, :], xx[:, k, cs],
                                                start=(k == 0 and n == 0), stop=(k == KD - 1 and n == 2))
                last.then_inc(lp_done, 1)

            over_chunks(pe, chunk)


def ffn_and_output(nc, sb, sem, passed, x_tok, xh, xl, o_dram, w13h, w13l, w2h, w2l, woh, wol, b13, lr, sh, sl,
                   a2, b2, out_tok):
    NR = len(FR)
    NI = CH // 128
    MT = NR * 4
    ctx = ExitStack()
    with ctx:
        oh, ol = xh[:, :, 0:CH], xl[:, :, 0:CH]
        hh, hl = xh[:, 0:NR, CH:2 * CH], xl[:, 0:NR, CH:2 * CH]
        num = sb(ctx, "num", [128, KD, CH])
        den = sb(ctx, "den", [128, KD, CH])
        on = sb(ctx, "on", [128, KD, CH])
        gate = sb(ctx, "gate", [128, 2, CH])
        hid = sb(ctx, "hid", [128, 4, CH])
        hsum = sb(ctx, "hsum", [128, 2, CH])
        z = sb(ctx, "z", [128, CH])
        xt = sb(ctx, "xt", [128, 2, D])
        gt = sb(ctx, "gt", [128, 2, D])
        res = sb(ctx, "res", [128, 2, D])
        gp = [ctx.enter_context(nc.psum_tensor(f"gp{i}", [128, CH], F32)) for i in range(2)]
        up = [ctx.enter_context(nc.psum_tensor(f"up{i}", [128, CH], F32)) for i in range(2)]
        zp = ctx.enter_context(nc.psum_tensor("zp", [128, CH], F32))
        yp = ctx.enter_context(nc.psum_tensor("yp", [128, D], F32))
        ap = [ctx.enter_context(nc.psum_tensor(f"ap{i}", [128, D], F32)) for i in range(2)]

        nd_loaded = sem("nd_loaded")
        xt_loaded = [sem(f"xt_loaded{i}") for i in range(2)]
        recip = sem("recip_done")
        on_done = sem("on_done")
        oh_done = sem("oh_done")
        ol_done = sem("ol_done")
        gate_done = sem("gate_done")
        up_done = sem("up_done")
        silu_done = sem("silu_done")
        hid_done = sem("hid_done")
        zmm_done = sem("zmm_done")
        hs_step = sem("hs_step")
        hh_done = sem("hh_done")
        hl_done = sem("hl_done")
        z_ready = sem("z_ready")
        y_done = sem("y_done")
        g_done = sem("g_done")
        a_done = sem("a_done")
        prod_done = sem("prod_done")
        res_done = sem("res_done")
        stored = [sem(f"stored{i}") for i in range(2)]
        block = ctx.enter_context(nc.Block())

        @block.sync
        def _(sp):
            def chunk(c):
                wait(sp, on_done, c)
                for kt in range(KD):
                    for n, dst in enumerate((num, den)):
                        sp.dma_start(dst[:, kt, :],
                                     o_dram[2 * kt:2 * kt + 2, :, bass.ds(c * CH, CH)]
                                     .rearrange("g (j r) n -> (g j) r n", j=SH)
                                     [:, 16 * n:16 * n + 16, :]).then_inc(nd_loaded, 16)
                wait(sp, res_done, c * NI)

                def load_xt(i):
                    sp.dma_start(xt[:, i % 2, :], x_tok[:, bass.ds(c * NI + i, 1), :]
                                 .rearrange("p a d -> p (a d)")).then_inc(xt_loaded[i % 2], 16)

                load_xt(0)
                load_xt(1)
                for i in range(NI):
                    hold(sp, passed, res_done, c * NI + i + 1)
                    sp.dma_start(out_tok[:, bass.ds(c * NI + i, 1), :].rearrange("p a d -> p (a d)"),
                                 res[:, i % 2, :]).then_inc(stored[i % 2], 16)
                    if i + 2 < NI:
                        load_xt(i + 2)

            over_chunks(sp, chunk)
            for i in range(2):
                sp.wait_ge(stored[i], 16 * NC * NI // 2)

        @block.gpsimd
        def _(pool):
            def chunk(c):
                for i in range(NI):
                    hold(pool, passed, xt_loaded[i % 2], 16 * (c * (NI // 2) + i // 2 + 1))
                    hold(pool, passed, prod_done, c * NI + i + 1)
                    nc.gpsimd.tensor_tensor(res[:, i % 2, :], res[:, i % 2, :], xt[:, i % 2, :], ALU.add).then_inc(res_done, 1)

            over_chunks(pool, chunk)

        def hi_part(act, c, r):
            n = FR[r]
            act.wait_ge(hs_step, (c * NR + r) * 3 + 3)
            if r == 0:
                wait(act, y_done, c * NI)
            nc.scalar.activation(hh[0:n, r, :], hsum[0:n, 1, :], ACT.Copy).then_inc(hh_done, 1)

        @block.scalar
        def _(act):
            def chunk(c):
                act.wait_ge(on_done, c + 1)
                wait(act, a_done, c * NI)
                nc.scalar.activation(oh, on[:, :, :], ACT.Copy).then_inc(oh_done, 1)
                for m in range(MT):
                    r = m // 4
                    n = FR[r]
                    act.wait_ge(gate_done, c * MT + m + 1)
                    if m >= 2:
                        act.wait_ge(hid_done, c * MT + m - 1)
                    else:
                        wait(act, hid_done, c * MT)
                    nc.scalar.activation(gate[0:n, m % 2, :], gp[m % 2][0:n, :], ACT.Silu).then_inc(silu_done, 1)
                    if m % 4 == 1 and m > 4:
                        hi_part(act, c, r - 1)
                hi_part(act, c, NR - 1)
                act.wait_ge(zmm_done, (c + 1) * NR)
                nc.scalar.activation(z[:, :], zp[:, :], ACT.Copy, scale=0.5).then_inc(z_ready, 1)
                for i in range(NI):
                    act.wait_ge(y_done, c * NI + i + 1)
                    if i >= 2:
                        act.wait_ge(prod_done, c * NI + i - 1)
                    else:
                        wait(act, prod_done, c * NI)
                    nc.scalar.activation(gt[:, i % 2, :], yp[:, :], ACT.Silu).then_inc(g_done, 1)

            over_chunks(act, chunk)

        @block.vector
        def _(dve):
            def chunk(c):
                dve.wait_ge(nd_loaded, (c + 1) * 16 * 2 * KD)
                wait(dve, ol_done, c)
                nc.vector.reciprocal(den[:, :, :], den[:, :, :]).then_inc(recip, 1)
                dve.wait_ge(recip, c + 1)
                nc.vector.tensor_tensor(on[:, :, :], num[:, :, :], den[:, :, :], ALU.mult).then_inc(on_done, 1)
                for m in range(MT):
                    r, j = m // 4, m % 4
                    n = FR[r]
                    dve.wait_ge(silu_done, c * MT + m + 1)
                    dve.wait_ge(up_done, c * MT + m + 1)
                    if j == 0:
                        wait(dve, zmm_done, c * NR + r)
                    nc.vector.tensor_tensor(hid[0:n, j, :], up[m % 2][0:n, :], gate[0:n, m % 2, :],
                                            ALU.mult).then_inc(hid_done, 1)
                    if j >= 1:
                        dve.wait_ge(hid_done, c * MT + m + 1)
                        step = (c * NR + r) * 3 + j
                        if j > 1:
                            dve.wait_ge(hs_step, step - 1)
                        else:
                            wait(dve, hl_done, c * NR + r)
                        src = hid[0:n, 0, :] if j == 1 else hsum[0:n, (j - 1) % 2, :]
                        nc.vector.tensor_tensor(hsum[0:n, j % 2, :], src, hid[0:n, j, :], ALU.add).then_inc(hs_step, 1)
                    if j == 3:
                        dve.wait_ge(hh_done, c * NR + r + 1)
                        nc.vector.tensor_tensor(hl[0:n, r, :], hsum[0:n, 1, :], hh[0:n, r, :],
                                                ALU.subtract).then_inc(hl_done, 1)
                    if m == 1:
                        dve.wait_ge(oh_done, c + 1)
                        nc.vector.tensor_tensor(ol, on[:, :, :], oh, ALU.subtract).then_inc(ol_done, 1)
                for i in range(NI):
                    dve.wait_ge(g_done, c * NI + i + 1)
                    dve.wait_ge(a_done, c * NI + i + 1)
                    if i < 2:
                        wait(dve, stored[i % 2], 16 * (c * (NI // 2)))
                    else:
                        dve.wait_ge(stored[i % 2], 16 * (c * (NI // 2) + 1))
                    nc.vector.tensor_tensor(res[:, i % 2, :], ap[i % 2][:, :], gt[:, i % 2, :],
                                            ALU.mult).then_inc(prod_done, 1)

            over_chunks(dve, chunk)

        @block.tensor
        def _(pe):
            def chunk(c):
                cs = bass.ds(c * CH, CH)

                def low_rank(r):
                    n = FR[r]
                    pe.wait_ge(hid_done, c * MT + 4 * r + 4)
                    if r == 0:
                        wait(pe, z_ready, c)
                    for j in range(4):
                        last = nc.tensor.matmul(zp[32 * j:32 * j + 32, :], a2[0:n, r, j, :], hid[0:n, j, :],
                                                start=(r == 0), stop=(r == NR - 1), tile_position=(0, 32 * j))
                    last.then_inc(zmm_done, 1)

                def attn_out(i):
                    if i >= 2:
                        pe.wait_ge(prod_done, c * NI + i - 1)
                    else:
                        wait(pe, prod_done, c * NI)
                    for k in range(KD):
                        for n, (o, w) in enumerate(((oh, woh), (oh, wol), (ol, woh))):
                            last = nc.tensor.matmul(ap[i % 2][:, :], o[:, k, i * 128:(i + 1) * 128], w[:, k, :],
                                                    start=(k == 0 and n == 0), stop=(k == KD - 1 and n == 2))
                    last.then_inc(a_done, 1)

                for m in range(MT):
                    r, j = m // 4, m % 4
                    n = FR[r]
                    lo = FB * j + 128 * r
                    for w, (dst, done) in enumerate(((gp, gate_done), (up, up_done))):
                        if m >= 2:
                            pe.wait_ge(hid_done, c * MT + m - 1)
                        else:
                            wait(pe, hid_done, c * MT)
                        nc.tensor.matmul(dst[m % 2][0:n, :], w13h[:, w, lo:lo + n], sh[:, cs], start=True, stop=False)
                        nc.tensor.matmul(dst[m % 2][0:n, :], w13h[:, w, lo:lo + n], sl[:, cs], start=False, stop=False)
                        nc.tensor.matmul(dst[m % 2][0:n, :], w13l[:, w, lo:lo + n], sh[:, cs], start=False, stop=False)
                        nc.tensor.matmul(dst[m % 2][0:n, :], b13[:, w, lo:lo + n], lr[:, cs],
                                         start=False, stop=True).then_inc(done, 1)
                    if m in (4, 8):
                        low_rank(r - 1)
                pe.wait_ge(ol_done, c + 1)
                attn_out(0)
                attn_out(1)
                low_rank(NR - 1)
                pe.wait_ge(hl_done, (c + 1) * NR)
                pe.wait_ge(z_ready, c + 1)
                for i in range(NI):
                    ts = slice(i * 128, (i + 1) * 128)
                    if i >= 1:
                        pe.wait_ge(g_done, c * NI + i)
                    else:
                        wait(pe, g_done, c * NI)
                    for r in range(NR):
                        n = FR[r]
                        for q, (h, w) in enumerate(((hh, w2h), (hh, w2l), (hl, w2h))):
                            nc.tensor.matmul(yp[:, :], h[0:n, r, ts], w[0:n, r, :],
                                             start=(r == 0 and q == 0), stop=False)
                    nc.tensor.matmul(yp[:, :], z[:, ts], b2[:, :], start=False, stop=True).then_inc(y_done, 1)
                    if i + 2 < NI:
                        attn_out(i + 2)

            over_chunks(pe, chunk)


_INS = ["x", "Wq_down", "Wq_up", "Wq_rope", "Wkv_down", "Wk_up", "Wv_up", "Wk_rope", "Wo"]
_FFN = ["w1q", "a1", "b1", "w3q", "a3", "b3", "w2q", "a2", "b2"]


def kernel(**inputs):
    import numpy as _np
    import concourse.bacc as _bacc
    from concourse import mybir as _mybir
    from concourse.bass_utils import run_bass_kernel_spmd as _run

    nc = _bacc.Bacc("TRN2", target_bir_lowering=False, num_devices=1)
    arrays, args = {}, {}

    def give(name, a):
        a = _np.ascontiguousarray(a)
        arrays[name] = a
        args[name] = nc.dram_tensor(name, a.shape, _mybir.dt.from_np(a.dtype), kind="ExternalInput").ap()

    for name in _INS:
        a = _np.asarray(inputs["L0_attn_" + name])
        if name == "Wq_rope":
            a = a.reshape(KD, 128, G, SH, NS, ROPE).transpose(2, 4, 1, 0, 3, 5).reshape(G, NS, 128, KD * SH * ROPE)
        elif name in ("Wq_up", "Wk_up"):
            a = a.reshape(LAT, G, SH, NS, HD).transpose(0, 1, 3, 2, 4).reshape(LAT, H * HD)
        give("in_" + name, a)
    for name in _FFN:
        give("in_" + name + "T", _np.asarray(inputs["L0_ffn_" + name]).T)
    shape = inputs["L0_attn_x"].shape
    out = nc.dram_tensor("out_dram", shape, _mybir.dt.float32, kind="ExternalOutput").ap()
    a = args
    attn_ffn_layer(nc, a["in_x"], a["in_Wq_down"], a["in_Wq_up"], a["in_Wq_rope"], a["in_Wkv_down"],
                   a["in_Wk_up"], a["in_Wv_up"], a["in_Wk_rope"], a["in_Wo"],
                   a["in_w1qT"], a["in_a1T"], a["in_b1T"], a["in_w3qT"], a["in_a3T"], a["in_b3T"],
                   a["in_w2qT"], a["in_a2T"], a["in_b2T"], out)
    r = _run(nc, [arrays], core_ids=[0])
    return r.results[0]["out_dram"]
```

```python
import concourse.bass as bass
from concourse import mybir
from contextlib import ExitStack

F32 = mybir.dt.float32
F32R = mybir.dt.float32r
ALU = mybir.AluOpType
ACT = mybir.ActivationFunctionType
AX = mybir.AxisListType

B, S, D = 8, 256, 512
T = B * S
H, HD, LAT, ROPE = 128, 4, 64, 64
KD = D // 128
GH = 16
G = H // GH
SH = 4
NS = GH // SH
NT = G * B
SCALE = float(HD + ROPE) ** -0.5
FF = 1376
RANK = 2
FB = FF // 4
FR = [128, 128, FB - 256]
CH = 512
NC = T // CH
EPS = 1e-5


def hold(eng, passed, semaphore, value):
    eng.wait_ge(semaphore, value)
    eng.sem_inc(passed, 1)


def wait(eng, semaphore, value):
    if not (isinstance(value, int) and value <= 0):
        eng.wait_ge(semaphore, value)


def over_chunks(eng, body):
    body(0)
    with eng.Fori(1, NC) as c:
        body(c)


def over_chunks_more(eng, body):
    body(0, True)
    with eng.Fori(1, NC - 1) as c:
        body(c, True)
    body(NC - 1, False)


def load_attention(sp, o_dram, num, den, c, nd_loaded):
    for kt in range(KD):
        for n, dst in enumerate((num, den)):
            sp.dma_start(dst[:, kt, :],
                         o_dram[2 * kt:2 * kt + 2, :, bass.ds(c * CH, CH)]
                         .rearrange("g (j r) n -> (g j) r n", j=SH)[:, 16 * n:16 * n + 16, :]).then_inc(nd_loaded, 16)


def attn_ffn_layer(nc, x, wq_down, wq_up, wq_rope, wkv_down, wk_up, wv_up, wk_rope, wo,
                   w1qT, a1T, b1T, w3qT, a3T, b3T, w2qT, a2T, b2T, out):
    v_dram = nc.dram_tensor("v_scratch", [T, H * HD], F32, kind="Internal").ap()
    o_dram = nc.dram_tensor("o_scratch", [G, 128, T], F32, kind="Internal").ap()
    x_tok = x.rearrange("b s d -> (b s) d").rearrange("(n p) d -> p n d", p=128)
    out_tok = out.rearrange("b s d -> (b s) d").rearrange("(n p) d -> p n d", p=128)

    top = ExitStack()
    with top:
        def sb(ctx, name, shape, dt=F32):
            return ctx.enter_context(nc.sbuf_tensor(name, shape, dt))

        def sem(name):
            return top.enter_context(nc.semaphore(name))

        xh = sb(top, "xh", [128, KD, T], F32R)
        xl = sb(top, "xl", [128, KD, T], F32R)
        passed = sem("passed")
        attn = ExitStack()
        with attn:
            cT = sb(attn, "cT", [128, T])
            krh = sb(attn, "krh", [128, T], F32R)
            krlh = sb(attn, "krlh", [128, T], F32R)
            w_stage = sb(attn, "w_stage", [128, NS, KD, SH * ROPE])
            wh = sb(attn, "wh", [128, NS, KD, SH * ROPE], F32R)
            wl = sb(attn, "wl", [128, NS, KD, SH * ROPE], F32R)
            up_all = sb(attn, "up_all", [128, G, 128])
            ident = sb(attn, "ident", [128, 128])

            w_staged = [sem(f"w_staged{s}") for s in range(NS)]
            w_hi = sem("w_hi")
            w_ready = sem("w_ready")
            project_inputs(nc, sb, sem, passed, x_tok, wq_down, wkv_down, wk_rope, wv_up, wq_up, wk_up, v_dram,
                           xh, xl, cT, krh, krlh, up_all, ident, w_stage, wh, wl, wq_rope, w_staged, w_hi, w_ready)
            attention(nc, sb, sem, passed, xh, xl, cT, krh, krlh, w_stage, wh, wl, wq_rope, w_staged, w_hi,
                      w_ready, up_all, ident, v_dram, o_dram)
        finish(nc, sb, sem, passed, x_tok, xh, xl, o_dram, wo, w1qT, a1T, b1T, w3qT, a3T, b3T, w2qT, a2T, b2T,
               out_tok)


def project_inputs(nc, sb, sem, passed, x_tok, wq_down, wkv_down, wk_rope, wv_up, wq_up, wk_up, v_dram,
                   xh, xl, cT, krh, krlh, up_all, ident, w_stage, wh, wl, wq_rope, w_staged, w_hi, w_ready):
    NTL = CH // 128
    ctx = ExitStack()
    with ctx:
        x_in = sb(ctx, "x_in", [128, T // 128, D])
        xn = sb(ctx, "xn", [128, NTL, D])
        stats = sb(ctx, "stats", [128, NTL, 6])
        mv = sb(ctx, "mv", [128, NTL, 2])
        var = sb(ctx, "var", [128, NTL])
        std = sb(ctx, "std", [128, NTL])
        rs = sb(ctx, "rs", [128, 4, NTL])
        ws = sb(ctx, "ws", [128, KD, 256])
        wsh = sb(ctx, "wsh", [128, KD, 256], F32R)
        wsl = sb(ctx, "wsl", [128, KD, 256], F32R)
        wv = sb(ctx, "wv", [128, H * HD])
        cc = sb(ctx, "cc", [128, CH])
        vs = sb(ctx, "vs", [128, NTL, H * HD])
        tp = [ctx.enter_context(nc.psum_tensor(f"tp{i}", [128, 512], F32)) for i in range(2)]
        cp = ctx.enter_context(nc.psum_tensor("cp", [128, CH], F32))
        kp = ctx.enter_context(nc.psum_tensor("kp", [128, CH], F32))
        vp = [ctx.enter_context(nc.psum_tensor(f"vp{i}", [128, 512], F32)) for i in range(2)]

        x_loaded = [sem(f"x_loaded{c}") for c in range(NC)]
        small_loaded = sem("small_loaded")
        up_loaded = sem("up_loaded")
        zeroed = sem("zeroed")
        ident_ready = sem("ident_ready")
        ws_hi = sem("ws_hi")
        ws_ready = sem("ws_ready")
        dve_step = sem("dve_step")
        var_ready = sem("var_ready")
        std_ready = sem("std_ready")
        xn_ready = sem("xn_ready")
        transposed = sem("transposed")
        xh_done = sem("xh_done")
        xl_done = sem("xl_done")
        c_done = sem("c_done")
        kr_done = sem("kr_done")
        cc_ready = sem("cc_ready")
        krh_done = sem("krh_done")
        krl_done = sem("krl_done")
        v_done = sem("v_done")
        vs_ready = sem("vs_ready")
        v_stored = sem("v_stored")

        def chunks(eng, body, loaded=None):
            body(0, True)
            if loaded is not None:
                for n in range(1, NC):
                    eng.wait_ge(loaded[n], 16)
            with eng.Fori(1, NC) as c:
                body(c, False)

        block = ctx.enter_context(nc.Block())

        @block.sync
        def _(sp):
            sp.dma_start(x_in[:, 0:NTL, :], x_tok[:, 0:NTL, :]).then_inc(x_loaded[0], 16)
            sp.dma_start(ws[:, :, 0:64], wq_down.rearrange("(k p) n -> p k n", p=128)).then_inc(small_loaded, 16)
            sp.dma_start(ws[:, :, 64:128], wkv_down.rearrange("(k p) n -> p k n", p=128)).then_inc(small_loaded, 16)
            sp.dma_start(ws[:, :, 128:192], wk_rope.rearrange("(k p) n -> p k n", p=128)).then_inc(small_loaded, 16)
            sp.dma_start(ws[:, :, 192:256], wk_rope.rearrange("(k p) n -> p k n", p=128)).then_inc(small_loaded, 16)
            sp.dma_start(wv[64:128, :], wv_up).then_inc(small_loaded, 16)
            for c in range(1, NC):
                sp.dma_start(x_in[:, c * NTL:(c + 1) * NTL, :],
                             x_tok[:, c * NTL:(c + 1) * NTL, :]).then_inc(x_loaded[c], 16)
            sp.wait_ge(zeroed, 2)
            sp.dma_start(up_all[0:64, :, 0:64], wq_up.rearrange("p (g n) -> p g n", g=G)).then_inc(up_loaded, 16)
            sp.dma_start(up_all[64:128, :, 64:128], wk_up.rearrange("p (g n) -> p g n", g=G)).then_inc(up_loaded, 16)
            for s in range(NS):
                sp.dma_start(w_stage[:, s], wq_rope[0, s].rearrange("p (k n) -> p k n", k=KD)).then_inc(w_staged[s], 16)
            def chunk(c):
                hold(sp, passed, vs_ready, (c + 1) * NTL)
                sp.dma_start(v_dram[bass.ds(c * CH, CH), :].rearrange("(n p) d -> p n d", p=128),
                             vs[:, :, :]).then_inc(v_stored, 16)

            over_chunks(sp, chunk)
            sp.wait_ge(v_stored, 16 * NC)
            sp.wait_ge(up_loaded, 32)

        @block.gpsimd
        def _(pool):
            nc.gpsimd.memset(ident[:, :], 0.0).then_inc(zeroed, 1)
            nc.gpsimd.memset(up_all[:, :, :], 0.0).then_inc(zeroed, 1)
            pool.wait_ge(zeroed, 2)
            nc.gpsimd.affine_select(out=ident[:, :], in_=ident[:, :], compare_op=ALU.not_equal, fill=1.0,
                                    base=0, pattern=[[-1, 128]], channel_multiplier=1).then_inc(ident_ready, 1)
            pool.wait_ge(ident_ready, 1)
            for s in range(NS):
                pool.wait_ge(w_staged[s], 16)
                nc.gpsimd.tensor_copy(wh[:, s], w_stage[:, s]).then_inc(w_hi, 1)
                pool.wait_ge(w_hi, s + 1)
                nc.gpsimd.tensor_tensor(wl[:, s], w_stage[:, s], wh[:, s], ALU.subtract).then_inc(w_ready, 1)

        @block.scalar
        def _(act):
            act.wait_ge(small_loaded, 80)
            nc.scalar.activation(wsh[:, :, :], ws[:, :, :], ACT.Copy).then_inc(ws_hi, 1)
            def body(c, first):
                act.wait_ge(var_ready, c + 1)
                nc.scalar.activation(std[:, :], var[:, :], ACT.Sqrt).then_inc(std_ready, 1)
                for i in range(NTL):
                    act.wait_ge(transposed, c * NTL + i + 1)
                    nc.scalar.activation(xh[:, :, bass.ds(c * CH + i * 128, 128)],
                                         tp[i % 2][:, :].rearrange("p (k n) -> p k n", k=KD),
                                         ACT.Copy).then_inc(xh_done, 1)
                act.wait_ge(c_done, c + 1)
                wait(act, v_done, c * NTL)
                nc.scalar.activation(cc[:, :], cp[:, :], ACT.Copy).then_inc(cc_ready, 1)
                act.wait_ge(kr_done, c + 1)
                nc.scalar.activation(krh[:, bass.ds(c * CH, CH)], kp[:, :], ACT.Copy).then_inc(krh_done, 1)
                nc.scalar.activation(krlh[64:128, bass.ds(c * CH, CH)], kp[64:128, :], ACT.Copy).then_inc(krl_done, 1)
                act.wait_ge(cc_ready, c + 1)
                nc.scalar.activation(cT[:, bass.ds(c * CH, CH)], cc[:, :], ACT.Copy)
                for i in range(NTL):
                    act.wait_ge(v_done, c * NTL + i + 1)
                    if i == 0:
                        wait(act, v_stored, 16 * c)
                    nc.scalar.activation(vs[:, i, :], vp[i % 2][:, :], ACT.Copy).then_inc(vs_ready, 1)

            chunks(act, body)

        @block.vector
        def _(dve):
            def body(c, first):
                steps = [0]

                def link(ins):
                    steps[0] += 1
                    ins.then_inc(dve_step, 1)
                    hold(dve, passed, dve_step, c * 7 + steps[0])

                for i in range(NTL):
                    last = nc.vector.bn_stats(stats[:, i, :], x_in[:, bass.ds(c * NTL + i, 1), :].rearrange("p a d -> p (a d)"))
                link(last)
                for i in range(NTL):
                    last = nc.vector.bn_aggr(mv[:, i, :], stats[:, i, :])
                link(last)
                nc.vector.tensor_scalar(var[:, :], mv[:, :, 1], EPS, None, ALU.add).then_inc(var_ready, 1)
                dve.wait_ge(std_ready, c + 1)
                link(nc.vector.reciprocal(rs[:, 0, :], std[:, :]))
                link(nc.vector.tensor_tensor(rs[:, 1, :], rs[:, 0, :], rs[:, 0, :], ALU.mult))
                link(nc.vector.tensor_tensor(rs[:, 2, :], rs[:, 1, :], var[:, :], ALU.mult))
                link(nc.vector.tensor_scalar(rs[:, 1, :], rs[:, 2, :], -0.5, 1.5, ALU.mult, ALU.add))
                link(nc.vector.tensor_tensor(rs[:, 3, :], rs[:, 1, :], rs[:, 0, :], ALU.mult))
                wait(dve, transposed, c * NTL)
                for i in range(NTL):
                    nc.vector.tensor_scalar(xn[:, i, :], x_in[:, bass.ds(c * NTL + i, 1), :].rearrange("p a d -> p (a d)"),
                                            mv[:, i, 0:1], rs[:, 3, i:i + 1], ALU.subtract, ALU.mult).then_inc(xn_ready, 1)
                for i in range(NTL):
                    dve.wait_ge(xh_done, c * NTL + i + 1)
                    xs = bass.ds(c * CH + i * 128, 128)
                    nc.vector.tensor_tensor(xl[:, :, xs], tp[i % 2][:, :].rearrange("p (k n) -> p k n", k=KD),
                                            xh[:, :, xs], ALU.subtract).then_inc(xl_done, 1)
                if first:
                    dve.wait_ge(ws_hi, 1)
                    nc.vector.tensor_tensor(wsl[:, :, :], ws[:, :, :], wsh[:, :, :], ALU.subtract).then_inc(ws_ready, 1)
                dve.wait_ge(krh_done, c + 1)
                nc.vector.tensor_tensor(krlh[0:64, bass.ds(c * CH, CH)], kp[0:64, :],
                                        krh[0:64, bass.ds(c * CH, CH)], ALU.subtract).then_inc(krl_done, 1)

            dve.wait_ge(x_loaded[0], 16)
            chunks(dve, body, x_loaded)

        @block.tensor
        def _(pe):
            pe.wait_ge(ident_ready, 1)
            pe.wait_ge(small_loaded, 80)
            def chunk(c):
                for i in range(NTL):
                    pe.wait_ge(xn_ready, c * NTL + i + 1)
                    if i < 2:
                        wait(pe, xl_done, c * NTL)
                    else:
                        pe.wait_ge(xl_done, c * NTL + i - 1)
                    for k in range(KD):
                        last = nc.tensor.transpose(tp[i % 2][:, k * 128:(k + 1) * 128],
                                                   xn[:, i, k * 128:(k + 1) * 128], ident[:, :])
                    last.then_inc(transposed, 1)
                pe.wait_ge(xl_done, (c + 1) * NTL)
                pe.wait_ge(ws_ready, 1)
                xs = bass.ds(c * CH, CH)
                wait(pe, cc_ready, c)
                for dst, lo, done in ((cp, 0, c_done), (kp, 128, kr_done)):
                    if lo:
                        wait(pe, krl_done, 2 * c)
                    for k in range(KD):
                        for n, (w, xx) in enumerate(((wsh, xh), (wsh, xl), (wsl, xh))):
                            last = nc.tensor.matmul(dst[:, :], w[:, k, lo:lo + 128], xx[:, k, xs],
                                                    start=(k == 0 and n == 0), stop=(k == KD - 1 and n == 2))
                    last.then_inc(done, 1)
                pe.wait_ge(cc_ready, c + 1)
                for i in range(NTL):
                    if i < 2:
                        wait(pe, vs_ready, c * NTL)
                    else:
                        pe.wait_ge(vs_ready, c * NTL + i - 1)
                    nc.tensor.matmul(vp[i % 2][:, :], cc[64:128, i * 128:(i + 1) * 128], wv[64:128, :],
                                     start=True, stop=True).then_inc(v_done, 1)

            over_chunks(pe, chunk)


def attention(nc, sb, sem, passed, xh, xl, cT, krh, krlh, w_stage, wh, wl, wq_rope, w_staged, w_hi, w_ready,
              up_all, ident, v_dram, o_dram):
    KC = 64 + 3 * HD * SH
    ctx = ExitStack()
    with ctx:
        slot1 = sb(ctx, "slot1", [128, NS, SH, S], F32R)
        slot2 = sb(ctx, "slot2", [128, NS, SH, S], F32R)
        k1 = sb(ctx, "k1", [128, NS, S], F32R)
        k2 = sb(ctx, "k2", [128, NS, S], F32R)
        content = sb(ctx, "content", [128, 3, S], F32R)
        up = sb(ctx, "up", [128, 128])
        probs = sb(ctx, "probs", [128, 2, SH, S])
        v_it = sb(ctx, "v_it", [128, 2, 2, GH * HD])
        vx = sb(ctx, "vx", [128, NS, 2, SH, 32])
        mx = sb(ctx, "mx", [128, NS, SH * 2])
        mrow = sb(ctx, "mrow", [SH * 2, NS, 128], F32R)
        o_sb = sb(ctx, "o_sb", [128, S])

        st = ctx.enter_context(nc.psum_tensor("st", [128, 2, SH, S], F32))
        sx = ctx.enter_context(nc.psum_tensor("sx", [128, 2, 512], F32))
        pj = ctx.enter_context(nc.psum_tensor("pj", [128, 2, S], F32))
        ob = ctx.enter_context(nc.psum_tensor("ob", [128, 2, S], F32))

        init_done = sem("init_done")
        slot_zeroed = sem("slot_zeroed")
        up_ready = sem("up_ready")
        proj_done = sem("proj_done")
        qh_done = sem("qh_done")
        ql_done = sem("ql_done")
        s2_done = sem("s2_done")
        k_ready = sem("k_ready")
        content_done = sem("content_done")
        ct_hi = sem("ct_hi")
        ct_lo = sem("ct_lo")
        ct_copy = sem("ct_copy")
        ct_in = [sem(f"ct_in{s}") for s in range(NS)]
        smax_done = sem("smax_done")
        max_done = sem("max_done")
        mt_done = sem("mt_done")
        mrow_ready = sem("mrow_ready")
        mrow_in = [sem(f"mrow_in{s}") for s in range(NS)]
        st_done = sem("st_done")
        exp_done = sem("exp_done")
        v_loaded = sem("v_loaded")
        vx_ready = sem("vx_ready")
        av_done = sem("av_done")
        o_evac = sem("o_evac")
        o_stored = sem("o_stored")

        def iterations(eng, body):
            body(0, True, False, True)
            with eng.Fori(1, NT - 1) as t:
                body(t, False, False, True)
            body(NT - 1, False, False, False)
            body(NT, False, True, False)

        block = ctx.enter_context(nc.Block())

        @block.sync
        def _(sp):
            def load_content(tt, s):
                hold(sp, passed, ct_hi, tt + 1)
                hold(sp, passed, ct_lo, 2 * (tt + 1))
                hold(sp, passed, ct_copy, tt + 1)
                sp.dma_start(k1[64:KC, s, :].bitcast(F32),
                             content[64 + 16 * s:80 + 16 * s, :, :].bitcast(F32)).then_inc(ct_in[s], 16)
                for j in range(SH):
                    r = 64 + 12 * j
                    sp.dma_start(slot1[r:r + 12, s, j, :].bitcast(F32),
                                 content[16 * s + 4 * j:16 * s + 4 * j + 4, :, :].bitcast(F32)).then_inc(ct_in[s], 16)

            def load_v(tt, par):
                g, b = tt // B, tt % B
                sp.dma_start(v_it[:, bass.ds(par, 1), :, :].rearrange("p a k n -> p (a k) n"),
                             v_dram[bass.ds(b * S, S), bass.ds(g * (GH * HD), GH * HD)]
                             .rearrange("(k p) n -> p k n", p=128)).then_inc(v_loaded, 16)

            def store_o(tt):
                hold(sp, passed, o_evac, tt + 1)
                sp.dma_start(o_dram[bass.ds(tt // B, 1), :, bass.ds((tt % B) * S, S)]
                             .rearrange("a p n -> (a p) n"), o_sb[:, :]).then_inc(o_stored, 16)

            def max_row(tt, s, v):
                hold(sp, passed, mrow_ready, v + 1)
                sp.dma_start(slot1[112:113, s, :, :].bitcast(F32),
                             mrow[:, s, :].bitcast(F32)).then_inc(mrow_in[s], 16)

            def body(t, first, stage):
                for s in range(NS):
                    u = t * NS + s
                    if not first or s >= 2:
                        max_row(t, (s + 2) % NS, u - 2)
                    if not first or s >= 3:
                        hold(sp, passed, st_done, u * 2 - 4)
                    if s < NS - 1:
                        load_content(t, s + 1)
                    else:
                        load_content(t + 1, 0)
                        hold(sp, passed, vx_ready, t * NS + 1)
                        load_v(t + 1, (t + 1) % 2)
                        if not first:
                            store_o(t - 1)
                    if stage is not None:
                        hold(sp, passed, w_ready, stage * NS + s + 1)
                        sp.dma_start(w_stage[:, s], wq_rope[bass.ds(stage + 1, 1), s].rearrange("a p (k n) -> (a p) k n", k=KD)).then_inc(w_staged[s], 16)

            sp.sem_inc(o_stored, 16)
            sp.wait_ge(init_done, 6)
            sp.wait_ge(slot_zeroed, 1)
            load_v(0, 0)
            load_content(0, 0)
            body(0, True, 0)
            with sp.Fori(1, B) as b:
                body(b, False, None)
            with sp.Fori(1, G - 1) as g:
                body(g * B, False, g)
                with sp.Fori(1, B) as b:
                    body(g * B + b, False, None)
            with sp.Fori((G - 1) * B, NT - 1) as t:
                body(t, False, None)
            t = NT - 1
            for s in range(NS):
                u = t * NS + s
                max_row(t, (s + 2) % NS, u - 2)
                if s < NS - 1:
                    hold(sp, passed, st_done, u * 2 - 4)
                    load_content(t, s + 1)
                else:
                    store_o(t - 1)
            for s in range(2):
                max_row(NT, (s + 2) % NS, NT * NS + s - 2)
            store_o(NT - 1)
            sp.wait_ge(o_stored, 16 * (NT + 1))

        @block.gpsimd
        def _(pool):
            nc.gpsimd.memset(k1[:, :, :].bitcast(F32), -1.0).then_inc(init_done, 1)
            nc.gpsimd.memset(vx[:, :, :, :, :], 0.0).then_inc(init_done, 1)
            pool.wait_ge(init_done, 2)
            for s in range(NS):
                nc.gpsimd.memset(vx[:, s, :, :, 16 + 4 * s:20 + 4 * s], 1.0).then_inc(init_done, 1)

            def refill(g, s):
                hold(pool, passed, w_hi, g * NS + s + 1)
                nc.gpsimd.tensor_tensor(wl[:, s], w_stage[:, s], wh[:, s], ALU.subtract).then_inc(w_ready, 1)

            def copy_up(g):
                nc.gpsimd.tensor_copy(up[:, :], up_all[:, bass.ds(g, 1), :].rearrange("p a n -> p (a n)")).then_inc(up_ready, 1)

            def body(t, b, first, refill_g):
                if refill_g is not None:
                    hold(pool, passed, content_done, t + 1)
                    copy_up(refill_g)
                bs = bass.ds(b * S, S)
                for s in range(NS):
                    u = t * NS + s
                    if not first:
                        hold(pool, passed, st_done, u * 2 - 6)
                    nc.gpsimd.tensor_copy(k1[0:64, s, :], krh[0:64, bs]).then_inc(k_ready, 1)
                    nc.gpsimd.tensor_copy(k2[:, s, :], krlh[:, bs]).then_inc(k_ready, 1)
                    if not first:
                        hold(pool, passed, av_done, u - 3)
                    if s == 0:
                        hold(pool, passed, v_loaded, 16 * (t + 1))
                    nc.gpsimd.tensor_copy(
                        vx[:, s, :, :, 4 * s:4 * s + 4],
                        v_it[:, bass.ds(t % 2, 1)].rearrange("p a k (j r) -> p (a k) j r", j=SH)
                        [:, :, :, 4 * s:4 * s + 4]).then_inc(vx_ready, 1)
                    if s == NS - 1:
                        content_copies(t + 1)
                    if refill_g is not None:
                        refill(refill_g, s)

            def content_copies(tt):
                hold(pool, passed, ct_hi, tt + 1)
                nc.gpsimd.tensor_copy(content[0:64, 2, :], content[0:64, 0, :]).then_inc(ct_copy, 1)

            copy_up(0)
            content_copies(0)
            body(0, 0, True, None)
            with pool.Fori(1, B - 1) as b:
                body(b, b, False, None)
            body(B - 1, B - 1, False, 1)
            with pool.Fori(1, G - 1) as g:
                with pool.Fori(0, B - 1) as b:
                    body(g * B + b, b, False, None)
                body(g * B + (B - 1), B - 1, False, g + 1)
            with pool.Fori(0, B - 1) as b:
                body(b + (G - 1) * B, b, False, None)
            t = NT - 1
            for s in range(NS):
                u = t * NS + s
                hold(pool, passed, st_done, u * 2 - 6)
                nc.gpsimd.tensor_copy(k1[0:64, s, :], krh[0:64, (B - 1) * S:B * S]).then_inc(k_ready, 1)
                nc.gpsimd.tensor_copy(k2[:, s, :], krlh[:, (B - 1) * S:B * S]).then_inc(k_ready, 1)
                hold(pool, passed, av_done, u - 3)
                if s == 0:
                    hold(pool, passed, v_loaded, 16 * (t + 1))
                nc.gpsimd.tensor_copy(
                    vx[:, s, :, :, 4 * s:4 * s + 4],
                    v_it[:, t % 2].rearrange("p k (j r) -> p k j r", j=SH)[:, :, :, 4 * s:4 * s + 4]).then_inc(vx_ready, 1)

        @block.scalar
        def _(act):
            def content_hi(tt):
                act.wait_ge(content_done, tt + 1)
                nc.scalar.activation(content[64:128, 1, :], ob[64:128, 1, :], ACT.Copy)
                nc.scalar.activation(content[:, 0, :], ob[:, 1, :], ACT.Copy).then_inc(ct_hi, 1)

            def body(t, first, last, more, refill_g):
                for s in range(NS if not last else 3):
                    u = t * NS + s
                    has_v = not first or s >= 3
                    if s == NS - 1 and not first:
                        act.wait_ge(av_done, t * NS)
                        act.wait_ge(o_stored, 16 * t)
                        nc.scalar.activation(o_sb[:, :], ob[:, 0, :], ACT.Copy).then_inc(o_evac, 1)
                    for kt in range(2):
                        if has_v:
                            v = u - 3
                            act.wait_ge(st_done, 2 * v + kt + 1)
                            if kt == 0 and not (first and s == 3):
                                act.wait_ge(av_done, v)
                            nc.scalar.activation(probs[:, kt], st[:, kt], ACT.Exp, scale=SCALE).then_inc(exp_done, 1)
                        if s == NS - 1 and kt == 0 and more:
                            for n in range(NS):
                                act.wait_ge(ct_in[n], 80 * (t + 1))
                            content_hi(t + 1)
                    if not last:
                        act.wait_ge(proj_done, u + 1)
                        if not first:
                            act.wait_ge(st_done, u * 2 - 6)
                        for e in range(2):
                            nc.scalar.activation(slot1[0:64, s, e:SH:2, :], pj[64 * e:64 * e + 64, :, :],
                                                 ACT.Copy).then_inc(qh_done, 1)
                    if refill_g is not None:
                        act.wait_ge(w_staged[s], 16 * (refill_g + 1))
                        nc.scalar.activation(wh[:, s], w_stage[:, s], ACT.Copy).then_inc(w_hi, 1)

            content_hi(0)
            act.wait_ge(init_done, 6)
            act.wait_ge(slot_zeroed, 1)
            body(0, True, False, True, None)
            with act.Fori(1, B - 1) as b:
                body(b, False, False, True, None)
            body(B - 1, False, False, True, 1)
            with act.Fori(1, G - 1) as g:
                with act.Fori(0, B - 1) as b:
                    body(g * B + b, False, False, True, None)
                body(g * B + (B - 1), False, False, True, g + 1)
            with act.Fori(0, B - 1) as b:
                body(b + (G - 1) * B, False, False, True, None)
            body(NT - 1, False, False, False, None)
            body(NT, False, True, False, None)
            act.wait_ge(av_done, NT * NS)
            act.wait_ge(o_stored, 16 * NT)
            nc.scalar.activation(o_sb[:, :], ob[:, 0, :], ACT.Copy).then_inc(o_evac, 1)

        @block.vector
        def _(dve):
            def content_lo(tt):
                dve.wait_ge(ct_hi, tt + 1)
                for lo, piece in ((0, 1), (64, 2)):
                    nc.vector.tensor_tensor(content[lo:lo + 64, piece, :], ob[lo:lo + 64, 1, :],
                                            content[lo:lo + 64, 0, :], ALU.subtract).then_inc(ct_lo, 1)

            def body(t, first, last, more):
                for s in range(NS if not last else 2):
                    u = t * NS + s
                    if not first or s >= 2:
                        sv = (s + 2) % NS
                        dve.wait_ge(mt_done, u - 1)
                        nc.vector.tensor_copy(mrow[:, sv, :], sx[0:SH * 2, 0, 0:128]).then_inc(mrow_ready, 1)
                    if (not first or s >= 1) and not (last and s >= 1):
                        dve.wait_ge(qh_done, 2 * u)
                        sv = (s + 3) % NS
                        nc.vector.tensor_copy(slot2[0:64, sv, :, :], slot1[0:64, sv, :, :]).then_inc(s2_done, 1)
                    if (not first or s >= 1) and not (last and s >= 1):
                        v, sv = u - 1, (s + 3) % NS
                        for j in range(SH):
                            if j == 2 and s == NS - 1 and more:
                                content_lo(t + 1)
                            dve.wait_ge(smax_done, v * SH + j + 1)
                            nc.vector.tensor_reduce(mx[:, sv, 2 * j:2 * j + 2],
                                                    sx[:, j % 2, :].rearrange("p (a k) -> p a k", a=2),
                                                    axis=AX.X, op=ALU.max).then_inc(max_done, 1)
                    if not last:
                        for e in range(2):
                            dve.wait_ge(qh_done, 2 * u + e + 1)
                            nc.vector.tensor_tensor(slot2[64:128, s, e:SH:2, :], pj[64 * e:64 * e + 64, :, :],
                                                    slot1[0:64, s, e:SH:2, :], ALU.subtract).then_inc(ql_done, 1)

            nc.vector.memset(slot1[:, :, :, :].bitcast(F32), 0.0).then_inc(slot_zeroed, 1)
            content_lo(0)
            iterations(dve, body)

        @block.tensor
        def _(pe):
            def content_product(tt):
                pe.wait_ge(up_ready, tt // B + 1)
                nc.tensor.matmul(ob[:, 1, :], up[:, :], cT[:, bass.ds((tt % B) * S, S)],
                                 start=True, stop=True).then_inc(content_done, 1)

            def transpose_max(s, v):
                pe.wait_ge(max_done, v * SH + SH)
                nc.tensor.transpose(sx[0:SH * 2, 0, 0:128], mx[:, s, :], ident[:, :]).then_inc(mt_done, 1)

            def scores(s, v, first, between=None):
                pe.wait_ge(ql_done, 2 * v + 2)
                pe.wait_ge(s2_done, v + 1)
                for kt in range(2):
                    ks = slice(kt * 128, kt * 128 + 128)
                    if not first:
                        pe.wait_ge(exp_done, 2 * v - 1 + kt)
                    for n, (kk, q, rows) in enumerate(((k1, slot1, KC + 1), (k2, slot2, 128))):
                        for hf in range(2):
                            last = nc.tensor.matmul(st[:, kt, 2 * hf:2 * hf + 2, :], kk[0:rows, s, ks],
                                                    q[0:rows, s, 2 * hf:2 * hf + 2, :],
                                                    start=(n == 0), stop=(n == 1))
                    last.then_inc(st_done, 1)
                    if kt == 0 and between is not None:
                        transpose_max(*between)

            def row_scores(s, v, j, first):
                if j >= 2 or not first:
                    pe.wait_ge(max_done, v * SH + j - 1)
                for qt in range(2):
                    last = nc.tensor.matmul(sx[:, j % 2, qt * S:(qt + 1) * S],
                                            slot1[0:KC, s, j, qt * 128:qt * 128 + 128], k1[0:KC, s, :],
                                            start=True, stop=True)
                last.then_inc(smax_done, 1)

            def project(t, s, bs):
                for p in range(2):
                    for k in range(KD):
                        for n, (w, xx) in enumerate(((wh, xh), (wh, xl), (wl, xh))):
                            last = nc.tensor.matmul(pj[:, p, :], w[:, s, k, 128 * p:128 * p + 128], xx[:, k, bs],
                                                    start=(k == 0 and n == 0), stop=(k == KD - 1 and n == 2))
                last.then_inc(proj_done, 1)

            def values(s, v):
                for kt in range(2):
                    for j in range(SH):
                        last = nc.tensor.matmul(ob[32 * j:32 * j + 32, 0, :], vx[:, s, kt, j, :], probs[:, kt, j, :],
                                                start=(s == 0 and kt == 0), stop=(s == NS - 1 and kt == 1),
                                                tile_position=(0, 32 * j))
                last.then_inc(av_done, 1)

            def body(t, first, last, more):
                bs = bass.ds((t % B) * S, S)
                for s in range(NS if not last else 3):
                    u = t * NS + s
                    has_v3 = not first or s >= 3
                    has_v1 = (not first or s >= 1) and not (last and s >= 1)
                    s3, s1 = (s + 1) % NS, (s + 3) % NS
                    if has_v3:
                        v = u - 3
                        tv = t if s == 3 else t - 1
                        pe.wait_ge(mrow_in[s3], 16 * (tv + 1))
                        scores(s3, v, first, ((s + 2) % NS, u - 2) if not last or s < 2 else None)
                    elif first and s == 2:
                        transpose_max(0, 0)
                    if s == NS - 1:
                        if not first:
                            pe.wait_ge(o_evac, t)
                        if more:
                            content_product(t + 1)
                    if has_v1:
                        v = u - 1
                        tv = t if s >= 1 else t - 1
                        pe.wait_ge(qh_done, 2 * v + 2)
                        pe.wait_ge(ct_in[s1], 80 * (tv + 1))
                        pe.wait_ge(k_ready, 2 * v + 2)
                        if not (first and s == 1):
                            pe.wait_ge(mrow_ready, v)
                        row_scores(s1, v, 0, first and s == 1)
                        row_scores(s1, v, 1, first and s == 1)
                    if not last:
                        pe.wait_ge(w_ready, (t // B) * NS + s + 1)
                        if not (first and s == 0):
                            pe.wait_ge(ql_done, 2 * u)
                        project(t, s, bs)
                    if has_v1:
                        row_scores(s1, u - 1, 2, False)
                        row_scores(s1, u - 1, 3, False)
                    if has_v3:
                        v = u - 3
                        pe.wait_ge(exp_done, 2 * v + 2)
                        pe.wait_ge(vx_ready, v + 1)
                        if s == NS - 1 and more:
                            pe.wait_ge(ct_lo, 2 * (t + 2))
                        values(s3, v)

            pe.wait_ge(init_done, 6)
            pe.wait_ge(slot_zeroed, 1)
            content_product(0)
            pe.wait_ge(ct_lo, 2)
            iterations(pe, body)


def finish(nc, sb, sem, passed, x_tok, xh, xl, o_dram, wo, w1qT, a1T, b1T, w3qT, a3T, b3T, w2qT, a2T, b2T, out_tok):
    ctx = ExitStack()
    with ctx:
        NR = len(FR)
        w13h = sb(ctx, "w13h", [128, 2, FF], F32R)
        w13l = sb(ctx, "w13l", [128, 2, FF], F32R)
        w2h = sb(ctx, "w2h", [128, NR, D], F32R)
        w2l = sb(ctx, "w2l", [128, NR, D], F32R)
        woh = sb(ctx, "woh", [128, KD, D], F32R)
        wol = sb(ctx, "wol", [128, KD, D], F32R)
        b13 = sb(ctx, "b13", [96, 2, FF], F32R)
        lr = sb(ctx, "lr", [96, T], F32R)
        sh = sb(ctx, "sh", [128, T], F32R)
        sl = sb(ctx, "sl", [128, T], F32R)
        a2 = sb(ctx, "a2", [128, NR, 4, 32])
        b2 = sb(ctx, "b2", [128, D])
        num = sb(ctx, "num", [128, KD, CH])
        den = sb(ctx, "den", [128, KD, CH])
        nd_loaded = sem("nd_loaded")
        recip = sem("recip_done")

        setup_ffn(nc, sb, sem, passed, xh, xl, wo, w1qT, a1T, b1T, w3qT, a3T, b3T, w2qT, a2T, b2T,
                  w13h, w13l, w2h, w2l, woh, wol, b13, lr, sh, sl, a2, b2, o_dram, num, den, nd_loaded, recip)
        ffn_and_output(nc, sb, sem, passed, x_tok, xh, xl, o_dram, w13h, w13l, w2h, w2l, woh, wol, b13, lr, sh, sl,
                       a2, b2, num, den, nd_loaded, recip, out_tok)


def setup_ffn(nc, sb, sem, passed, xh, xl, wo, w1qT, a1T, b1T, w3qT, a3T, b3T, w2qT, a2T, b2T,
              w13h, w13l, w2h, w2l, woh, wol, b13, lr, sh, sl, a2, b2, o_dram, num, den, nd_loaded, recip):
    NR = len(FR)
    FH = FF // 2
    ctx = ExitStack()
    with ctx:
        raw13 = sb(ctx, "raw13", [128, 2, FF])
        raw2 = sb(ctx, "raw2", [128, NR, D])
        rawo = sb(ctx, "rawo", [128, KD, D])
        rawb = sb(ctx, "rawb", [96, 2, FH])
        rawa = sb(ctx, "rawa", [128, KD, 2 * RANK])
        la = sb(ctx, "la", [128, KD, 96])
        lah = sb(ctx, "lah", [128, KD, 96], F32R)
        lal = sb(ctx, "lal", [128, KD, 96], F32R)
        one = sb(ctx, "one", [128, 128])
        oner = sb(ctx, "oner", [128, 128], F32R)
        lrt = sb(ctx, "lrt", [96, CH], F32R)
        sp_ = ctx.enter_context(nc.psum_tensor("sump", [128, CH], F32))
        lp = ctx.enter_context(nc.psum_tensor("lp", [96, CH], F32))

        loaded = [sem(f"fl{i}") for i in range(5)]
        zeroed = sem("f_zeroed")
        pads = sem("f_pads")
        eye = sem("f_eye")
        la_ready = sem("f_la_ready")
        la_hi = sem("f_la_hi")
        la_split = sem("f_la_split")
        hi = sem("f_hi")
        lo = sem("f_lo")
        sum_done = sem("f_sum_done")
        lp_done = sem("f_lp_done")
        sh_done = sem("f_sh_done")
        sl_done = sem("f_sl_done")
        lrh_done = sem("f_lrh_done")
        lr_done = sem("f_lr_done")
        b_zero = sem("f_b_zero")
        b_hi = sem("f_b_hi")
        b_lo = sem("f_b_lo")
        block = ctx.enter_context(nc.Block())

        @block.sync
        def _(sp):
            sp.dma_start(rawa[:, :, 0:RANK], a1T.rearrange("(k p) n -> p k n", p=128)).then_inc(loaded[0], 16)
            sp.dma_start(rawa[:, :, RANK:2 * RANK], a3T.rearrange("(k p) n -> p k n", p=128)).then_inc(loaded[0], 16)
            sp.dma_start(raw13[:, 0, :], w1qT).then_inc(loaded[1], 16)
            sp.dma_start(raw13[:, 1, :], w3qT).then_inc(loaded[1], 16)
            sp.dma_start(raw2[:, 0:2, :], w2qT[0:256, :].rearrange("(k p) n -> p k n", p=128)).then_inc(loaded[2], 16)
            sp.dma_start(raw2[0:FR[2], 2, :], w2qT[256:FB, :]).then_inc(loaded[2], 16)
            sp.dma_start(rawo[:, :, :], wo.rearrange("(k p) n -> p k n", p=128)).then_inc(loaded[2], 16)
            load_attention(sp, o_dram, num, den, 0, nd_loaded)
            sp.wait_ge(b_zero, 1)
            for hf in range(2):
                wait(sp, b_lo, hf)
                for r in (0, 32, 64):
                    sp.dma_start(rawb[r:r + RANK, 0, :], b1T[:, hf * FH:(hf + 1) * FH]).then_inc(loaded[4], 16)
                    sp.dma_start(rawb[r + RANK:r + 2 * RANK, 1, :], b3T[:, hf * FH:(hf + 1) * FH]).then_inc(loaded[4], 16)
            sp.wait_ge(zeroed, 4)
            for r in range(NR):
                sp.dma_start(a2[0:FR[r], r, :, 0:RANK],
                             a2T.rearrange("(j p) n -> p j n", j=4)[128 * r:128 * r + FR[r], :, :]).then_inc(pads, 16)
            for j in range(4):
                sp.dma_start(b2[32 * j:32 * j + RANK, :], b2T).then_inc(pads, 16)
            sp.wait_ge(pads, 16 * 7)

        @block.gpsimd
        def _(pool):
            nc.gpsimd.memset(rawb[:, :, :], 0.0).then_inc(b_zero, 1)
            nc.gpsimd.memset(one[:, :], 0.0).then_inc(zeroed, 1)
            nc.gpsimd.memset(la[:, :, :], 0.0).then_inc(zeroed, 1)
            nc.gpsimd.memset(a2[:, :, :, :], 0.0).then_inc(zeroed, 1)
            nc.gpsimd.memset(b2[:, :], 0.0).then_inc(zeroed, 1)
            pool.wait_ge(zeroed, 4)
            nc.gpsimd.affine_select(out=one[:, :], in_=one[:, :], compare_op=ALU.not_equal, fill=1.0,
                                    base=0, pattern=[[-1, 128]], channel_multiplier=1).then_inc(eye, 1)
            pool.wait_ge(loaded[0], 32)
            for c in (0, 32, 64):
                nc.gpsimd.tensor_copy(la[:, :, c:c + 2 * RANK], rawa[:, :, :]).then_inc(la_ready, 1)
            pool.wait_ge(hi, 2)
            nc.gpsimd.tensor_tensor(w2l[:, 0:2, :], raw2[:, 0:2, :], w2h[:, 0:2, :], ALU.subtract)
            nc.gpsimd.tensor_tensor(w2l[0:FR[2], 2, :], raw2[0:FR[2], 2, :], w2h[0:FR[2], 2, :], ALU.subtract)
            nc.gpsimd.tensor_tensor(wol[:, :, :], rawo[:, :, :], woh[:, :, :], ALU.subtract).then_inc(lo, 1)

        @block.scalar
        def _(act):
            act.wait_ge(eye, 1)
            nc.scalar.activation(oner[:, :], one[:, :], ACT.Copy).then_inc(la_hi, 1)
            act.wait_ge(la_ready, 3)
            nc.scalar.activation(lah[:, :, :], la[:, :, :], ACT.Copy).then_inc(la_hi, 1)

            def b_hi_part(hf):
                act.wait_ge(loaded[4], 96 * (hf + 1))
                nc.scalar.activation(b13[:, :, hf * FH:(hf + 1) * FH], rawb[:, :, :], ACT.Copy).then_inc(b_hi, 1)

            act.wait_ge(loaded[1], 32)
            nc.scalar.activation(w13h[:, :, :], raw13[:, :, :], ACT.Copy).then_inc(hi, 1)
            def chunk(c):
                cs = bass.ds(c * CH, CH)
                act.wait_ge(sum_done, c + 1)
                nc.scalar.activation(sh[:, cs], sp_[:, :], ACT.Copy).then_inc(sh_done, 1)
                act.wait_ge(lp_done, c + 1)
                wait(act, lr_done, c)
                nc.scalar.activation(lr[0:64, cs], lp[0:64, :], ACT.Copy, scale=0.5)
                nc.scalar.activation(lrt[64:96, :], lp[64:96, :], ACT.Copy, scale=0.5).then_inc(lrh_done, 1)

            chunk(0)
            act.wait_ge(loaded[2], 48)
            nc.scalar.activation(w2h[:, 0:2, :], raw2[:, 0:2, :], ACT.Copy)
            nc.scalar.activation(w2h[0:FR[2], 2, :], raw2[0:FR[2], 2, :], ACT.Copy)
            nc.scalar.activation(woh[:, :, :], rawo[:, :, :], ACT.Copy).then_inc(hi, 1)
            chunk(1)
            b_hi_part(0)
            chunk(2)
            b_hi_part(1)
            chunk(3)

        @block.vector
        def _(dve):
            dve.wait_ge(la_hi, 2)
            nc.vector.tensor_tensor(lal[:, :, :], la[:, :, :], lah[:, :, :], ALU.subtract).then_inc(la_split, 1)
            dve.wait_ge(hi, 1)
            nc.vector.tensor_tensor(w13l[:, :, :], raw13[:, :, :], w13h[:, :, :], ALU.subtract).then_inc(lo, 1)
            def chunk(c):
                cs = bass.ds(c * CH, CH)
                dve.wait_ge(sh_done, c + 1)
                nc.vector.tensor_tensor(sl[:, cs], sp_[:, :], sh[:, cs], ALU.subtract).then_inc(sl_done, 1)
                dve.wait_ge(lrh_done, c + 1)
                nc.vector.scalar_tensor_tensor(out=lr[64:96, cs], in0=lp[64:96, :], scalar=0.5, in1=lrt[64:96, :],
                                               op0=ALU.mult, op1=ALU.subtract).then_inc(lr_done, 1)

            def b_lo_part(hf):
                dve.wait_ge(b_hi, hf + 1)
                fs = slice(hf * FH, (hf + 1) * FH)
                nc.vector.tensor_tensor(b13[32:64, :, fs], rawb[32:64, :, :], b13[32:64, :, fs],
                                        ALU.subtract).then_inc(b_lo, 1)

            def reciprocals(kts):
                for kt in kts:
                    nc.vector.reciprocal(den[:, kt, :], den[:, kt, :]).then_inc(recip, 1)

            chunk(0)
            dve.wait_ge(nd_loaded, 16 * 2 * KD)
            reciprocals((0,))
            chunk(1)
            reciprocals((1,))
            b_lo_part(0)
            chunk(2)
            reciprocals((2,))
            b_lo_part(1)
            chunk(3)
            reciprocals((3,))

        @block.tensor
        def _(pe):
            pe.wait_ge(la_hi, 1)
            def chunk(c, first=False):
                cs = bass.ds(c * CH, CH)
                wait(pe, sl_done, c)
                for k in range(KD):
                    for xx in (xh, xl):
                        last = nc.tensor.matmul(sp_[:, :], oner[:, :], xx[:, k, cs],
                                                start=(k == 0 and xx is xh), stop=(k == KD - 1 and xx is xl))
                last.then_inc(sum_done, 1)
                if first:
                    pe.wait_ge(la_hi, 2)
                    pe.wait_ge(la_split, 1)
                wait(pe, lr_done, c)
                for k in range(KD):
                    for n, (w, xx) in enumerate(((lah, xh), (lah, xl), (lal, xh))):
                        last = nc.tensor.matmul(lp[:, :], w[:, k, :], xx[:, k, cs],
                                                start=(k == 0 and n == 0), stop=(k == KD - 1 and n == 2))
                last.then_inc(lp_done, 1)

            chunk(0, True)
            with pe.Fori(1, NC) as c:
                chunk(c)


def ffn_and_output(nc, sb, sem, passed, x_tok, xh, xl, o_dram, w13h, w13l, w2h, w2l, woh, wol, b13, lr, sh, sl,
                   a2, b2, num, den, nd_loaded, recip, out_tok):
    NR = len(FR)
    NI = CH // 128
    MT = NR * 4
    ctx = ExitStack()
    with ctx:
        oh, ol = xh[:, :, 0:CH], xl[:, :, 0:CH]
        hh, hl = xh[:, 0:NR, CH:2 * CH], xl[:, 0:NR, CH:2 * CH]
        gate = sb(ctx, "gate", [128, 2, CH])
        hid = sb(ctx, "hid", [128, 2, 4, CH])
        hsum = sb(ctx, "hsum", [128, 2, CH])
        z = sb(ctx, "z", [128, CH])
        xt = sb(ctx, "xt", [128, 2, D])
        gt = sb(ctx, "gt", [128, 2, D])
        res = sb(ctx, "res", [128, 2, D])
        gp = [ctx.enter_context(nc.psum_tensor(f"gp{i}", [128, CH], F32)) for i in range(2)]
        up = [ctx.enter_context(nc.psum_tensor(f"up{i}", [128, CH], F32)) for i in range(2)]
        zp = ctx.enter_context(nc.psum_tensor("zp", [128, CH], F32))
        yp = [ctx.enter_context(nc.psum_tensor("yp", [128, D], F32)), zp]
        ap = [ctx.enter_context(nc.psum_tensor(f"ap{i}", [128, D], F32)) for i in range(2)]

        xt_loaded = [sem(f"xt_loaded{i}") for i in range(2)]
        on_done = sem("on_done")
        oh_done = sem("oh_done")
        ol_done = sem("ol_done")
        gate_done = sem("gate_done")
        up_done = sem("up_done")
        silu_done = sem("silu_done")
        hid_done = sem("hid_done")
        zmm_done = sem("zmm_done")
        hs_step = sem("hs_step")
        hh_done = sem("hh_done")
        hl_done = sem("hl_done")
        z_ready = sem("z_ready")
        y_done = sem("y_done")
        g_done = sem("g_done")
        a_done = sem("a_done")
        prod_done = sem("prod_done")
        res_done = sem("res_done")
        stored = [sem(f"stored{i}") for i in range(2)]
        block = ctx.enter_context(nc.Block())

        @block.sync
        def _(sp):
            def chunk(c, more):
                def load_xt(i):
                    sp.dma_start(xt[:, i % 2, :], x_tok[:, bass.ds(c * NI + i, 1), :]
                                 .rearrange("p a d -> p (a d)")).then_inc(xt_loaded[i % 2], 16)

                wait(sp, res_done, c * NI)
                load_xt(0)
                load_xt(1)
                if more:
                    hold(sp, passed, ol_done, (c + 1) * KD)
                    load_attention(sp, o_dram, num, den, c + 1, nd_loaded)
                for i in range(NI):
                    hold(sp, passed, res_done, c * NI + i + 1)
                    sp.dma_start(out_tok[:, bass.ds(c * NI + i, 1), :].rearrange("p a d -> p (a d)"),
                                 res[:, i % 2, :]).then_inc(stored[i % 2], 16)
                    if i + 2 < NI:
                        load_xt(i + 2)

            over_chunks_more(sp, chunk)
            for i in range(2):
                sp.wait_ge(stored[i], 16 * NC * NI // 2)

        @block.gpsimd
        def _(pool):
            def normalise(c, kt):
                hold(pool, passed, recip, c * KD + kt + 1)
                nc.gpsimd.tensor_tensor(num[:, kt, :], num[:, kt, :], den[:, kt, :], ALU.mult).then_inc(on_done, 1)

            def chunk(c, more):
                for i in range(NI):
                    if more:
                        normalise(c + 1, i)
                    hold(pool, passed, xt_loaded[i % 2], 16 * (c * (NI // 2) + i // 2 + 1))
                    hold(pool, passed, prod_done, c * NI + i + 1)
                    nc.gpsimd.tensor_tensor(res[:, i % 2, :], res[:, i % 2, :], xt[:, i % 2, :], ALU.add).then_inc(res_done, 1)

            for kt in range(KD):
                normalise(0, kt)
            over_chunks_more(pool, chunk)

        def hi_part(act, c, r):
            n = FR[r]
            act.wait_ge(hs_step, (c * NR + r) * 3 + 3)
            if r == 0:
                wait(act, y_done, c * NI)
            nc.scalar.activation(hh[0:n, r, :], hsum[0:n, 1, :], ACT.Copy).then_inc(hh_done, 1)

        @block.scalar
        def _(act):
            def chunk(c):
                for m in range(MT):
                    r = m // 4
                    n = FR[r]
                    act.wait_ge(gate_done, c * MT + m + 1)
                    if m >= 2:
                        act.wait_ge(hid_done, c * MT + m - 1)
                    else:
                        wait(act, hid_done, c * MT)
                    nc.scalar.activation(gate[0:n, m % 2, :], gp[m % 2][0:n, :], ACT.Silu).then_inc(silu_done, 1)
                    if 2 <= m < 2 + KD:
                        act.wait_ge(on_done, c * KD + m - 1)
                        if m == 2:
                            wait(act, a_done, c * NI)
                        nc.scalar.activation(oh[:, m - 2, :], num[:, m - 2, :], ACT.Copy).then_inc(oh_done, 1)
                    if m % 4 == 1 and m > 4:
                        hi_part(act, c, r - 1)
                hi_part(act, c, NR - 1)
                act.wait_ge(zmm_done, (c + 1) * NR)
                nc.scalar.activation(z[:, :], zp[:, :], ACT.Copy, scale=0.5).then_inc(z_ready, 1)
                for i in range(NI):
                    act.wait_ge(y_done, c * NI + i + 1)
                    if i >= 2:
                        act.wait_ge(prod_done, c * NI + i - 1)
                    else:
                        wait(act, prod_done, c * NI)
                    nc.scalar.activation(gt[:, i % 2, :], yp[i % 2][:, :], ACT.Silu).then_inc(g_done, 1)

            over_chunks(act, chunk)

        @block.vector
        def _(dve):
            def chunk(c, more):
                for m in range(MT):
                    r, j = m // 4, m % 4
                    n = FR[r]
                    dve.wait_ge(silu_done, c * MT + m + 1)
                    dve.wait_ge(up_done, c * MT + m + 1)
                    if j == 0:
                        wait(dve, zmm_done, c * NR + max(r - 1, 0))
                    nc.vector.tensor_tensor(hid[0:n, r % 2, j, :], up[m % 2][0:n, :], gate[0:n, m % 2, :],
                                            ALU.mult).then_inc(hid_done, 1)
                    if j >= 1:
                        dve.wait_ge(hid_done, c * MT + m + 1)
                        step = (c * NR + r) * 3 + j
                        if j > 1:
                            dve.wait_ge(hs_step, step - 1)
                        else:
                            wait(dve, hl_done, c * NR + r)
                        src = hid[0:n, r % 2, 0, :] if j == 1 else hsum[0:n, (j - 1) % 2, :]
                        nc.vector.tensor_tensor(hsum[0:n, j % 2, :], src, hid[0:n, r % 2, j, :], ALU.add).then_inc(hs_step, 1)
                    if j == 3:
                        dve.wait_ge(hh_done, c * NR + r + 1)
                        nc.vector.tensor_tensor(hl[0:n, r, :], hsum[0:n, 1, :], hh[0:n, r, :],
                                                ALU.subtract).then_inc(hl_done, 1)
                    if 3 <= m < 3 + KD:
                        dve.wait_ge(oh_done, c * KD + m - 2)
                        nc.vector.tensor_tensor(ol[:, m - 3, :], num[:, m - 3, :], oh[:, m - 3, :],
                                                ALU.subtract).then_inc(ol_done, 1)
                for i in range(NI):
                    if more:
                        if i == 0:
                            dve.wait_ge(nd_loaded, (c + 2) * 16 * 2 * KD)
                        nc.vector.reciprocal(den[:, i, :], den[:, i, :]).then_inc(recip, 1)
                    dve.wait_ge(g_done, c * NI + i + 1)
                    dve.wait_ge(a_done, c * NI + i + 1)
                    if i < 2:
                        wait(dve, stored[i % 2], 16 * (c * (NI // 2)))
                    else:
                        dve.wait_ge(stored[i % 2], 16 * (c * (NI // 2) + 1))
                    nc.vector.tensor_tensor(res[:, i % 2, :], ap[i % 2][:, :], gt[:, i % 2, :],
                                            ALU.mult).then_inc(prod_done, 1)

            over_chunks_more(dve, chunk)

        @block.tensor
        def _(pe):
            def chunk(c):
                cs = bass.ds(c * CH, CH)

                def low_rank(r):
                    n = FR[r]
                    pe.wait_ge(hid_done, c * MT + 4 * r + 4)
                    if r == 0:
                        wait(pe, g_done, c * NI)
                    for j in range(4):
                        last = nc.tensor.matmul(zp[32 * j:32 * j + 32, :], a2[0:n, r, j, :], hid[0:n, r % 2, j, :],
                                                start=(r == 0), stop=(r == NR - 1), tile_position=(0, 32 * j))
                    last.then_inc(zmm_done, 1)

                def attn_out(i):
                    if i >= 2:
                        pe.wait_ge(prod_done, c * NI + i - 1)
                    else:
                        wait(pe, prod_done, c * NI)
                    for k in range(KD):
                        for n, (o, w) in enumerate(((oh, woh), (oh, wol), (ol, woh))):
                            last = nc.tensor.matmul(ap[i % 2][:, :], o[:, k, i * 128:(i + 1) * 128], w[:, k, :],
                                                    start=(k == 0 and n == 0), stop=(k == KD - 1 and n == 2))
                    last.then_inc(a_done, 1)

                for m in range(MT):
                    r, j = m // 4, m % 4
                    n = FR[r]
                    lo = FB * j + 128 * r
                    for w, (dst, done) in enumerate(((gp, gate_done), (up, up_done))):
                        if m >= 2:
                            pe.wait_ge(hid_done, c * MT + m - 1)
                        else:
                            wait(pe, hid_done, c * MT)
                        nc.tensor.matmul(dst[m % 2][0:n, :], w13h[:, w, lo:lo + n], sh[:, cs], start=True, stop=False)
                        nc.tensor.matmul(dst[m % 2][0:n, :], w13h[:, w, lo:lo + n], sl[:, cs], start=False, stop=False)
                        nc.tensor.matmul(dst[m % 2][0:n, :], w13l[:, w, lo:lo + n], sh[:, cs], start=False, stop=False)
                        nc.tensor.matmul(dst[m % 2][0:n, :], b13[:, w, lo:lo + n], lr[:, cs],
                                         start=False, stop=True).then_inc(done, 1)
                    if m in (5, 9):
                        low_rank(r - 1)
                pe.wait_ge(ol_done, (c + 1) * KD)
                attn_out(0)
                low_rank(NR - 1)
                attn_out(1)
                pe.wait_ge(hl_done, (c + 1) * NR)
                pe.wait_ge(z_ready, c + 1)
                for i in range(NI):
                    ts = slice(i * 128, (i + 1) * 128)
                    if i >= 2:
                        pe.wait_ge(g_done, c * NI + i - 1)
                    else:
                        wait(pe, g_done, c * NI)
                    for r in range(NR):
                        n = FR[r]
                        for q, (h, w) in enumerate(((hh, w2h), (hh, w2l), (hl, w2h))):
                            nc.tensor.matmul(yp[i % 2][:, :], h[0:n, r, ts], w[0:n, r, :],
                                             start=(r == 0 and q == 0), stop=False)
                    nc.tensor.matmul(yp[i % 2][:, :], z[:, ts], b2[:, :], start=False, stop=True).then_inc(y_done, 1)
                    if 1 <= i < NI - 1:
                        attn_out(i + 1)

            over_chunks(pe, chunk)


_INS = ["x", "Wq_down", "Wq_up", "Wq_rope", "Wkv_down", "Wk_up", "Wv_up", "Wk_rope", "Wo"]
_FFN = ["w1q", "a1", "b1", "w3q", "a3", "b3", "w2q", "a2", "b2"]


def kernel(**inputs):
    import numpy as _np
    import concourse.bacc as _bacc
    from concourse import mybir as _mybir
    from concourse.bass_utils import run_bass_kernel_spmd as _run

    nc = _bacc.Bacc("TRN2", target_bir_lowering=False, num_devices=1)
    arrays, args = {}, {}

    def give(name, a):
        a = _np.ascontiguousarray(a)
        arrays[name] = a
        args[name] = nc.dram_tensor(name, a.shape, _mybir.dt.from_np(a.dtype), kind="ExternalInput").ap()

    for name in _INS:
        a = _np.asarray(inputs["L0_attn_" + name])
        if name == "Wq_rope":
            a = a.reshape(KD, 128, G, SH, NS, ROPE).transpose(2, 4, 1, 0, 3, 5).reshape(G, NS, 128, KD * SH * ROPE)
        elif name in ("Wq_up", "Wk_up"):
            a = a.reshape(LAT, G, SH, NS, HD).transpose(0, 1, 3, 2, 4).reshape(LAT, H * HD)
        give("in_" + name, a)
    for name in _FFN:
        give("in_" + name + "T", _np.asarray(inputs["L0_ffn_" + name]).T)
    shape = inputs["L0_attn_x"].shape
    out = nc.dram_tensor("out_dram", shape, _mybir.dt.float32, kind="ExternalOutput").ap()
    a = args
    attn_ffn_layer(nc, a["in_x"], a["in_Wq_down"], a["in_Wq_up"], a["in_Wq_rope"], a["in_Wkv_down"],
                   a["in_Wk_up"], a["in_Wv_up"], a["in_Wk_rope"], a["in_Wo"],
                   a["in_w1qT"], a["in_a1T"], a["in_b1T"], a["in_w3qT"], a["in_a3T"], a["in_b3T"],
                   a["in_w2qT"], a["in_a2T"], a["in_b2T"], out)
    r = _run(nc, [arrays], core_ids=[0])
    return r.results[0]["out_dram"]
```

```python
import concourse.bass as bass
from concourse import mybir
from contextlib import ExitStack

F32 = mybir.dt.float32
F32R = mybir.dt.float32r
ALU = mybir.AluOpType
ACT = mybir.ActivationFunctionType
AX = mybir.AxisListType

B, S, D = 8, 256, 512
T = B * S
H, HD, LAT, ROPE = 128, 4, 64, 64
KD = D // 128
GH = 16
G = H // GH
SH = 4
NS = GH // SH
NT = G * B
SCALE = float(HD + ROPE) ** -0.5
FF = 1376
RANK = 2
FB = FF // 4
FR = [128, 128, FB - 256]
CH = 512
NC = T // CH
EPS = 1e-5


def hold(eng, passed, semaphore, value):
    eng.wait_ge(semaphore, value)
    eng.sem_inc(passed, 1)


def wait(eng, semaphore, value):
    if not (isinstance(value, int) and value <= 0):
        eng.wait_ge(semaphore, value)


def over_chunks(eng, body):
    body(0)
    with eng.Fori(1, NC) as c:
        body(c)


def over_chunks_more(eng, body):
    body(0, True)
    with eng.Fori(1, NC - 1) as c:
        body(c, True)
    body(NC - 1, False)


def load_attention(sp, o_dram, dst, n, c, loaded):
    for kt in range(KD):
        sp.dma_start(dst[:, kt, :],
                     o_dram[2 * kt:2 * kt + 2, :, bass.ds(c * CH, CH)]
                     .rearrange("g (j r) n -> (g j) r n", j=SH)[:, 16 * n:16 * n + 16, :]).then_inc(loaded, 16)


def attn_ffn_layer(nc, x, wq_down, wq_up, wq_rope, wkv_down, wk_up, wv_up, wk_rope, wo,
                   w1qT, a1T, b1T, w3qT, a3T, b3T, w2qT, a2T, b2T, out):
    v_dram = nc.dram_tensor("v_scratch", [T, H * HD], F32, kind="Internal").ap()
    o_dram = nc.dram_tensor("o_scratch", [G, 128, T], F32, kind="Internal").ap()
    x_tok = x.rearrange("b s d -> (b s) d").rearrange("(n p) d -> p n d", p=128)
    out_tok = out.rearrange("b s d -> (b s) d").rearrange("(n p) d -> p n d", p=128)

    top = ExitStack()
    with top:
        def sb(ctx, name, shape, dt=F32):
            return ctx.enter_context(nc.sbuf_tensor(name, shape, dt))

        def sem(name):
            return top.enter_context(nc.semaphore(name))

        xh = sb(top, "xh", [128, KD, T], F32R)
        xl = sb(top, "xl", [128, KD, T], F32R)
        passed = sem("passed")
        attn = ExitStack()
        with attn:
            cT = sb(attn, "cT", [128, T])
            krh = sb(attn, "krh", [128, T], F32R)
            krlh = sb(attn, "krlh", [128, T], F32R)
            w_stage = sb(attn, "w_stage", [128, NS, KD, SH * ROPE])
            wh = sb(attn, "wh", [128, NS, KD, SH * ROPE], F32R)
            wl = sb(attn, "wl", [128, NS, KD, SH * ROPE], F32R)
            up_all = sb(attn, "up_all", [128, G, 128])
            ident = sb(attn, "ident", [128, 128])

            vs = sb(attn, "vs", [128, CH // 128, H * HD])
            v_stored = sem("v_stored")
            w_staged = [sem(f"w_staged{s}") for s in range(NS)]
            w_hi = sem("w_hi")
            w_ready = sem("w_ready")
            project_inputs(nc, sb, sem, passed, x_tok, wq_down, wkv_down, wk_rope, wv_up, wq_up, wk_up, v_dram,
                           xh, xl, cT, krh, krlh, up_all, ident, w_stage, wh, wl, wq_rope, w_staged, w_hi, w_ready,
                           vs, v_stored)
            attention(nc, sb, sem, passed, xh, xl, cT, krh, krlh, w_stage, wh, wl, wq_rope, w_staged, w_hi,
                      w_ready, up_all, ident, v_dram, o_dram, v_stored)
        finish(nc, sb, sem, passed, x_tok, xh, xl, o_dram, wo, w1qT, a1T, b1T, w3qT, a3T, b3T, w2qT, a2T, b2T,
               out_tok)


def project_inputs(nc, sb, sem, passed, x_tok, wq_down, wkv_down, wk_rope, wv_up, wq_up, wk_up, v_dram,
                   xh, xl, cT, krh, krlh, up_all, ident, w_stage, wh, wl, wq_rope, w_staged, w_hi, w_ready,
                   vs, v_stored):
    NTL = CH // 128
    ctx = ExitStack()
    with ctx:
        x_in = sb(ctx, "x_in", [128, T // 128, D])
        xn = sb(ctx, "xn", [128, NTL, D])
        stats = sb(ctx, "stats", [128, T // 128, 6])
        mv = sb(ctx, "mv", [128, T // 128, 2])
        var = sb(ctx, "var", [128, T // 128])
        std = sb(ctx, "std", [128, T // 128])
        rs = sb(ctx, "rs", [128, 4, T // 128])
        ws = sb(ctx, "ws", [128, KD, 256])
        wsh = sb(ctx, "wsh", [128, KD, 256], F32R)
        wsl = sb(ctx, "wsl", [128, KD, 256], F32R)
        wv = sb(ctx, "wv", [128, H * HD])
        cc = sb(ctx, "cc", [128, CH])
        tp = [ctx.enter_context(nc.psum_tensor(f"tp{i}", [128, 512], F32)) for i in range(2)]
        cp = ctx.enter_context(nc.psum_tensor("cp", [128, CH], F32))
        kp = ctx.enter_context(nc.psum_tensor("kp", [128, CH], F32))
        vp = [ctx.enter_context(nc.psum_tensor(f"vp{i}", [128, 512], F32)) for i in range(2)]

        x_loaded = [sem(f"x_loaded{c}") for c in range(NC)]
        small_loaded = sem("small_loaded")
        up_loaded = sem("up_loaded")
        zeroed = sem("zeroed")
        ident_ready = sem("ident_ready")
        ws_hi = sem("ws_hi")
        ws_ready = sem("ws_ready")
        dve_step = sem("dve_step")
        var_ready = sem("var_ready")
        std_ready = sem("std_ready")
        xn_ready = sem("xn_ready")
        transposed = sem("transposed")
        xh_done = sem("xh_done")
        xl_done = sem("xl_done")
        c_done = sem("c_done")
        kr_done = sem("kr_done")
        cc_ready = sem("cc_ready")
        krh_done = sem("krh_done")
        krl_done = sem("krl_done")
        v_done = sem("v_done")
        vs_ready = sem("vs_ready")

        def chunks(eng, body):
            body(0, True)
            with eng.Fori(1, NC - 1) as c:
                body(c, True)
            body(NC - 1, False)

        block = ctx.enter_context(nc.Block())

        @block.sync
        def _(sp):
            sp.dma_start(x_in[:, 0:NTL, :], x_tok[:, 0:NTL, :]).then_inc(x_loaded[0], 16)
            sp.dma_start(ws[:, :, 0:64], wq_down.rearrange("(k p) n -> p k n", p=128)).then_inc(small_loaded, 16)
            sp.dma_start(ws[:, :, 64:128], wkv_down.rearrange("(k p) n -> p k n", p=128)).then_inc(small_loaded, 16)
            sp.dma_start(ws[:, :, 128:192], wk_rope.rearrange("(k p) n -> p k n", p=128)).then_inc(small_loaded, 16)
            sp.dma_start(ws[:, :, 192:256], wk_rope.rearrange("(k p) n -> p k n", p=128)).then_inc(small_loaded, 16)
            sp.dma_start(wv[64:128, :], wv_up).then_inc(small_loaded, 16)
            for c in range(1, NC):
                sp.dma_start(x_in[:, c * NTL:(c + 1) * NTL, :],
                             x_tok[:, c * NTL:(c + 1) * NTL, :]).then_inc(x_loaded[c], 16)
            sp.wait_ge(zeroed, 2)
            sp.dma_start(up_all[0:64, :, 0:64], wq_up.rearrange("p (g n) -> p g n", g=G)).then_inc(up_loaded, 16)
            sp.dma_start(up_all[64:128, :, 64:128], wk_up.rearrange("p (g n) -> p g n", g=G)).then_inc(up_loaded, 16)
            for s in range(NS):
                sp.dma_start(w_stage[:, s], wq_rope[0, s].rearrange("p (k n) -> p k n", k=KD)).then_inc(w_staged[s], 16)
            def chunk(c):
                hold(sp, passed, vs_ready, (c + 1) * NTL)
                sp.dma_start(v_dram[bass.ds(c * CH, CH), :].rearrange("(n p) d -> p n d", p=128),
                             vs[:, :, :]).then_inc(v_stored, 16)

            over_chunks(sp, chunk)
            sp.wait_ge(up_loaded, 32)

        @block.gpsimd
        def _(pool):
            nc.gpsimd.memset(ident[:, :], 0.0).then_inc(zeroed, 1)
            nc.gpsimd.memset(up_all[:, :, :], 0.0).then_inc(zeroed, 1)
            pool.wait_ge(zeroed, 2)
            nc.gpsimd.affine_select(out=ident[:, :], in_=ident[:, :], compare_op=ALU.not_equal, fill=1.0,
                                    base=0, pattern=[[-1, 128]], channel_multiplier=1).then_inc(ident_ready, 1)
            pool.wait_ge(ident_ready, 1)
            pool.wait_ge(ws_hi, 1)
            nc.gpsimd.tensor_tensor(wsl[:, :, :], ws[:, :, :], wsh[:, :, :], ALU.subtract).then_inc(ws_ready, 1)
            for s in range(NS):
                pool.wait_ge(w_staged[s], 16)
                nc.gpsimd.tensor_copy(wh[:, s], w_stage[:, s]).then_inc(w_hi, 1)
                pool.wait_ge(w_hi, s + 1)
                nc.gpsimd.tensor_tensor(wl[:, s], w_stage[:, s], wh[:, s], ALU.subtract).then_inc(w_ready, 1)

        @block.scalar
        def _(act):
            def hi_transposed(c, i):
                act.wait_ge(transposed, c * NTL + i + 1)
                nc.scalar.activation(xh[:, :, bass.ds(c * CH + i * 128, 128)],
                                     tp[i % 2][:, :].rearrange("p (k n) -> p k n", k=KD),
                                     ACT.Copy).then_inc(xh_done, 1)

            def body(c, more):
                act.wait_ge(c_done, c + 1)
                wait(act, v_done, c * NTL)
                nc.scalar.activation(cc[:, :], cp[:, :], ACT.Copy).then_inc(cc_ready, 1)
                act.wait_ge(kr_done, c + 1)
                nc.scalar.activation(krh[:, bass.ds(c * CH, CH)], kp[:, :], ACT.Copy).then_inc(krh_done, 1)
                nc.scalar.activation(krlh[64:128, bass.ds(c * CH, CH)], kp[64:128, :], ACT.Copy).then_inc(krl_done, 1)
                act.wait_ge(cc_ready, c + 1)
                nc.scalar.activation(cT[:, bass.ds(c * CH, CH)], cc[:, :], ACT.Copy)
                for i in range(NTL):
                    if i % 2 == 0 and more:
                        hi_transposed(c + 1, i)
                        hi_transposed(c + 1, i + 1)
                    act.wait_ge(v_done, c * NTL + i + 1)
                    if i == 0:
                        wait(act, v_stored, 16 * c)
                    nc.scalar.activation(vs[:, i, :], vp[i % 2][:, :], ACT.Copy).then_inc(vs_ready, 1)

            act.wait_ge(var_ready, 1)
            nc.scalar.activation(std[:, 0:NTL], var[:, 0:NTL], ACT.Sqrt).then_inc(std_ready, 1)
            act.wait_ge(small_loaded, 80)
            nc.scalar.activation(wsh[:, :, :], ws[:, :, :], ACT.Copy).then_inc(ws_hi, 1)
            for i in range(NTL):
                hi_transposed(0, i)
            act.wait_ge(var_ready, 2)
            nc.scalar.activation(std[:, NTL:], var[:, NTL:], ACT.Sqrt).then_inc(std_ready, 1)
            chunks(act, body)

        @block.vector
        def _(dve):
            steps = [0]

            def link(ins):
                steps[0] += 1
                ins.then_inc(dve_step, 1)
                dve.wait_ge(dve_step, steps[0])

            def statistics(part, tiles):
                lo, hi = tiles
                ts = slice(lo, hi)
                for i in range(lo, hi):
                    if i % NTL == 0:
                        dve.wait_ge(x_loaded[i // NTL], 16)
                    last = nc.vector.bn_stats(stats[:, i, :], x_in[:, i, :])
                link(last)
                for i in range(lo, hi):
                    last = nc.vector.bn_aggr(mv[:, i, :], stats[:, i, :])
                link(last)
                nc.vector.tensor_scalar(var[:, ts], mv[:, ts, 1], EPS, None, ALU.add).then_inc(var_ready, 1)
                dve.wait_ge(std_ready, part + 1)
                link(nc.vector.reciprocal(rs[:, 0, ts], std[:, ts]))
                link(nc.vector.tensor_tensor(rs[:, 1, ts], rs[:, 0, ts], rs[:, 0, ts], ALU.mult))
                link(nc.vector.tensor_tensor(rs[:, 2, ts], rs[:, 1, ts], var[:, ts], ALU.mult))
                link(nc.vector.tensor_scalar(rs[:, 1, ts], rs[:, 2, ts], -0.5, 1.5, ALU.mult, ALU.add))
                link(nc.vector.tensor_tensor(rs[:, 3, ts], rs[:, 1, ts], rs[:, 0, ts], ALU.mult))

            def normalise(c):
                wait(dve, transposed, c * NTL)
                for i in range(NTL):
                    n = c * NTL + i
                    nc.vector.tensor_scalar(xn[:, i, :], x_in[:, bass.ds(n, 1), :].rearrange("p a d -> p (a d)"),
                                            mv[:, bass.ds(n, 1), 0:1].rearrange("p a o -> p (a o)"),
                                            rs[:, 3, bass.ds(n, 1)], ALU.subtract, ALU.mult).then_inc(xn_ready, 1)

            def lo_transposed(c, i):
                dve.wait_ge(xh_done, c * NTL + i + 1)
                xs = bass.ds(c * CH + i * 128, 128)
                nc.vector.tensor_tensor(xl[:, :, xs], tp[i % 2][:, :].rearrange("p (k n) -> p k n", k=KD),
                                        xh[:, :, xs], ALU.subtract).then_inc(xl_done, 1)

            def body(c, more):
                if more:
                    normalise(c + 1)
                dve.wait_ge(krh_done, c + 1)
                nc.vector.tensor_tensor(krlh[0:64, bass.ds(c * CH, CH)], kp[0:64, :],
                                        krh[0:64, bass.ds(c * CH, CH)], ALU.subtract).then_inc(krl_done, 1)
                if more:
                    for i in range(NTL):
                        lo_transposed(c + 1, i)

            statistics(0, (0, NTL))
            normalise(0)
            for i in range(NTL):
                lo_transposed(0, i)
            statistics(1, (NTL, T // 128))
            chunks(dve, body)

        @block.tensor
        def _(pe):
            pe.wait_ge(ident_ready, 1)
            pe.wait_ge(small_loaded, 80)
            def transpose(c, i):
                pe.wait_ge(xn_ready, c * NTL + i + 1)
                if i < 2:
                    wait(pe, xl_done, c * NTL)
                else:
                    pe.wait_ge(xl_done, c * NTL + i - 1)
                for k in range(KD):
                    last = nc.tensor.transpose(tp[i % 2][:, k * 128:(k + 1) * 128],
                                               xn[:, i, k * 128:(k + 1) * 128], ident[:, :])
                last.then_inc(transposed, 1)

            def body(c, more):
                pe.wait_ge(xl_done, (c + 1) * NTL)
                pe.wait_ge(ws_ready, 1)
                xs = bass.ds(c * CH, CH)
                wait(pe, cc_ready, c)
                for dst, lo, done in ((cp, 0, c_done), (kp, 128, kr_done)):
                    if lo:
                        wait(pe, krl_done, 2 * c)
                    for k in range(KD):
                        for n, (w, xx) in enumerate(((wsh, xh), (wsh, xl), (wsl, xh))):
                            last = nc.tensor.matmul(dst[:, :], w[:, k, lo:lo + 128], xx[:, k, xs],
                                                    start=(k == 0 and n == 0), stop=(k == KD - 1 and n == 2))
                    last.then_inc(done, 1)
                pe.wait_ge(cc_ready, c + 1)
                for i in range(NTL):
                    if i % 2 == 0 and more:
                        transpose(c + 1, i)
                        transpose(c + 1, i + 1)
                    if i < 2:
                        wait(pe, vs_ready, c * NTL)
                    else:
                        pe.wait_ge(vs_ready, c * NTL + i - 1)
                    nc.tensor.matmul(vp[i % 2][:, :], cc[64:128, i * 128:(i + 1) * 128], wv[64:128, :],
                                     start=True, stop=True).then_inc(v_done, 1)

            for i in range(NTL):
                transpose(0, i)
            chunks(pe, body)


def attention(nc, sb, sem, passed, xh, xl, cT, krh, krlh, w_stage, wh, wl, wq_rope, w_staged, w_hi, w_ready,
              up_all, ident, v_dram, o_dram, v_stored):
    KC = 64 + 3 * HD * SH
    ctx = ExitStack()
    with ctx:
        slot1 = sb(ctx, "slot1", [128, NS, SH, S], F32R)
        slot2 = sb(ctx, "slot2", [128, NS, SH, S], F32R)
        k1 = sb(ctx, "k1", [128, NS, S], F32R)
        k2 = sb(ctx, "k2", [128, S], F32R)
        content = sb(ctx, "content", [128, 3, S], F32R)
        up = sb(ctx, "up", [128, 128])
        probs = sb(ctx, "probs", [128, 2, SH, S])
        v_it = sb(ctx, "v_it", [128, 2, 2, GH * HD])
        vx = sb(ctx, "vx", [128, NS, 2, SH, 32])
        mx = sb(ctx, "mx", [128, NS, SH * 2])
        mrow = sb(ctx, "mrow", [SH * 2, NS, 128], F32R)
        o_sb = sb(ctx, "o_sb", [128, S])

        st = ctx.enter_context(nc.psum_tensor("st", [128, 2, SH, S], F32))
        sx = ctx.enter_context(nc.psum_tensor("sx", [128, 2, 512], F32))
        pj = ctx.enter_context(nc.psum_tensor("pj", [128, 2, S], F32))
        ob = ctx.enter_context(nc.psum_tensor("ob", [128, 2, S], F32))

        init_done = sem("init_done")
        slot_zeroed = [sem(f"slot_zeroed{i}") for i in range(2)]
        up_ready = sem("up_ready")
        proj_done = sem("proj_done")
        qh_done = sem("qh_done")
        ql_done = sem("ql_done")
        s2_done = sem("s2_done")
        k_ready = sem("k_ready")
        content_done = sem("content_done")
        ct_hi = sem("ct_hi")
        ct_lo = sem("ct_lo")
        ct_copy = sem("ct_copy")
        ct_in = [sem(f"ct_in{s}") for s in range(NS)]
        smax_done = sem("smax_done")
        max_done = sem("max_done")
        mt_done = sem("mt_done")
        mrow_ready = sem("mrow_ready")
        mrow_in = [sem(f"mrow_in{s}") for s in range(NS)]
        st_done = sem("st_done")
        exp_done = sem("exp_done")
        k2_ready = sem("k2_ready")
        v_loaded = sem("v_loaded")
        vx_ready = sem("vx_ready")
        av_done = sem("av_done")
        o_evac = sem("o_evac")
        o_stored = sem("o_stored")

        def iterations(eng, body):
            body(0, True, False, True)
            with eng.Fori(1, NT - 1) as t:
                body(t, False, False, True)
            body(NT - 1, False, False, False)
            body(NT, False, True, False)

        block = ctx.enter_context(nc.Block())

        @block.sync
        def _(sp):
            def load_content(tt, s):
                hold(sp, passed, ct_hi, tt + 1)
                hold(sp, passed, ct_lo, 2 * (tt + 1))
                hold(sp, passed, ct_copy, tt + 1)
                sp.dma_start(k1[64:KC, s, :].bitcast(F32),
                             content[64 + 16 * s:80 + 16 * s, :, :].bitcast(F32)).then_inc(ct_in[s], 16)
                for j in range(SH):
                    r = 64 + 12 * j
                    sp.dma_start(slot1[r:r + 12, s, j, :].bitcast(F32),
                                 content[16 * s + 4 * j:16 * s + 4 * j + 4, :, :].bitcast(F32)).then_inc(ct_in[s], 16)

            def load_v(tt, par):
                g, b = tt // B, tt % B
                sp.dma_start(v_it[:, bass.ds(par, 1), :, :].rearrange("p a k n -> p (a k) n"),
                             v_dram[bass.ds(b * S, S), bass.ds(g * (GH * HD), GH * HD)]
                             .rearrange("(k p) n -> p k n", p=128)).then_inc(v_loaded, 16)

            def store_o(tt):
                hold(sp, passed, o_evac, tt + 1)
                sp.dma_start(o_dram[bass.ds(tt // B, 1), :, bass.ds((tt % B) * S, S)]
                             .rearrange("a p n -> (a p) n"), o_sb[:, :]).then_inc(o_stored, 16)

            def max_row(tt, s, v):
                hold(sp, passed, mrow_ready, v + 1)
                sp.dma_start(slot1[112:113, s, :, :].bitcast(F32),
                             mrow[:, s, :].bitcast(F32)).then_inc(mrow_in[s], 16)

            def body(t, first, stage):
                for s in range(NS):
                    u = t * NS + s
                    if not first or s >= 2:
                        max_row(t, (s + 2) % NS, u - 2)
                    if not first or s >= 3:
                        hold(sp, passed, st_done, u * 2 - 4)
                    if s < NS - 1:
                        load_content(t, s + 1)
                    else:
                        load_content(t + 1, 0)
                        hold(sp, passed, vx_ready, t * NS + 1)
                        load_v(t + 1, (t + 1) % 2)
                        if not first:
                            store_o(t - 1)
                    if stage is not None:
                        hold(sp, passed, w_ready, stage * NS + s + 1)
                        sp.dma_start(w_stage[:, s], wq_rope[bass.ds(stage + 1, 1), s].rearrange("a p (k n) -> (a p) k n", k=KD)).then_inc(w_staged[s], 16)

            sp.sem_inc(o_stored, 16)
            sp.wait_ge(init_done, 6)
            for zeroed in slot_zeroed:
                sp.wait_ge(zeroed, 1)
            load_content(0, 0)
            sp.wait_ge(v_stored, 16 * NC)
            load_v(0, 0)
            body(0, True, 0)
            with sp.Fori(1, B) as b:
                body(b, False, None)
            with sp.Fori(1, G - 1) as g:
                body(g * B, False, g)
                with sp.Fori(1, B) as b:
                    body(g * B + b, False, None)
            with sp.Fori((G - 1) * B, NT - 1) as t:
                body(t, False, None)
            t = NT - 1
            for s in range(NS):
                u = t * NS + s
                max_row(t, (s + 2) % NS, u - 2)
                if s < NS - 1:
                    hold(sp, passed, st_done, u * 2 - 4)
                    load_content(t, s + 1)
                else:
                    store_o(t - 1)
            for s in range(2):
                max_row(NT, (s + 2) % NS, NT * NS + s - 2)
            store_o(NT - 1)
            sp.wait_ge(o_stored, 16 * (NT + 1))

        @block.gpsimd
        def _(pool):
            def copy_up(g):
                nc.gpsimd.tensor_copy(up[:, :], up_all[:, bass.ds(g, 1), :].rearrange("p a n -> p (a n)")).then_inc(up_ready, 1)

            copy_up(0)
            nc.gpsimd.memset(slot1[:, 2:4, :, :].bitcast(F32), 0.0).then_inc(slot_zeroed[1], 1)
            nc.gpsimd.memset(k1[:, :, :].bitcast(F32), -1.0).then_inc(init_done, 1)
            def content_copies(tt):
                hold(pool, passed, ct_hi, tt + 1)
                nc.gpsimd.tensor_copy(content[0:64, 2, :], content[0:64, 0, :]).then_inc(ct_copy, 1)

            content_copies(0)
            pool.wait_ge(ct_copy, 1)
            nc.gpsimd.memset(vx[:, :, :, :, :], 0.0).then_inc(init_done, 1)
            pool.wait_ge(init_done, 2)
            for s in range(NS):
                nc.gpsimd.memset(vx[:, s, :, :, 16 + 4 * s:20 + 4 * s], 1.0).then_inc(init_done, 1)

            def refill(g, s):
                hold(pool, passed, w_hi, g * NS + s + 1)
                nc.gpsimd.tensor_tensor(wl[:, s], w_stage[:, s], wh[:, s], ALU.subtract).then_inc(w_ready, 1)

            def body(t, b, first, refill_g):
                if refill_g is not None:
                    hold(pool, passed, content_done, t + 1)
                    copy_up(refill_g)
                bs = bass.ds(b * S, S)
                for s in range(NS):
                    u = t * NS + s
                    if not first:
                        hold(pool, passed, st_done, u * 2 - 6)
                    nc.gpsimd.tensor_copy(k1[0:64, s, :], krh[0:64, bs]).then_inc(k_ready, 1)
                    if not first:
                        hold(pool, passed, av_done, u - 3)
                    if s == 0:
                        hold(pool, passed, v_loaded, 16 * (t + 1))
                    nc.gpsimd.tensor_copy(
                        vx[:, s, :, :, 4 * s:4 * s + 4],
                        v_it[:, bass.ds(t % 2, 1)].rearrange("p a k (j r) -> p (a k) j r", j=SH)
                        [:, :, :, 4 * s:4 * s + 4]).then_inc(vx_ready, 1)
                    if s == 2:
                        if not first:
                            hold(pool, passed, st_done, t * NS * 2)
                        nc.gpsimd.tensor_copy(k2[:, :], krlh[:, bs]).then_inc(k2_ready, 1)
                    if s == NS - 1:
                        content_copies(t + 1)
                    if refill_g is not None:
                        refill(refill_g, s)

            body(0, 0, True, None)
            with pool.Fori(1, B - 1) as b:
                body(b, b, False, None)
            body(B - 1, B - 1, False, 1)
            with pool.Fori(1, G - 1) as g:
                with pool.Fori(0, B - 1) as b:
                    body(g * B + b, b, False, None)
                body(g * B + (B - 1), B - 1, False, g + 1)
            with pool.Fori(0, B - 1) as b:
                body(b + (G - 1) * B, b, False, None)
            t = NT - 1
            for s in range(NS):
                u = t * NS + s
                hold(pool, passed, st_done, u * 2 - 6)
                nc.gpsimd.tensor_copy(k1[0:64, s, :], krh[0:64, (B - 1) * S:B * S]).then_inc(k_ready, 1)
                if s == 2:
                    hold(pool, passed, st_done, t * NS * 2)
                    nc.gpsimd.tensor_copy(k2[:, :], krlh[:, (B - 1) * S:B * S]).then_inc(k2_ready, 1)
                hold(pool, passed, av_done, u - 3)
                if s == 0:
                    hold(pool, passed, v_loaded, 16 * (t + 1))
                nc.gpsimd.tensor_copy(
                    vx[:, s, :, :, 4 * s:4 * s + 4],
                    v_it[:, t % 2].rearrange("p k (j r) -> p k j r", j=SH)[:, :, :, 4 * s:4 * s + 4]).then_inc(vx_ready, 1)

        @block.scalar
        def _(act):
            def content_hi(tt):
                act.wait_ge(content_done, tt + 1)
                nc.scalar.activation(content[64:128, 1, :], ob[64:128, 1, :], ACT.Copy)
                nc.scalar.activation(content[:, 0, :], ob[:, 1, :], ACT.Copy).then_inc(ct_hi, 1)

            def body(t, first, last, more, refill_g):
                for s in range(NS if not last else 3):
                    u = t * NS + s
                    has_v = not first or s >= 3
                    if s == NS - 1 and not first:
                        act.wait_ge(av_done, t * NS)
                        act.wait_ge(o_stored, 16 * t)
                        nc.scalar.activation(o_sb[:, :], ob[:, 0, :], ACT.Copy).then_inc(o_evac, 1)
                    for kt in range(2):
                        if has_v:
                            v = u - 3
                            act.wait_ge(st_done, 2 * v + kt + 1)
                            if kt == 0 and not (first and s == 3):
                                act.wait_ge(av_done, v)
                            nc.scalar.activation(probs[:, kt], st[:, kt], ACT.Exp, scale=SCALE).then_inc(exp_done, 1)
                        if s == NS - 1 and kt == 0 and more:
                            for n in range(NS):
                                act.wait_ge(ct_in[n], 80 * (t + 1))
                            content_hi(t + 1)
                    if not last:
                        act.wait_ge(proj_done, u + 1)
                        if not first:
                            act.wait_ge(st_done, u * 2 - 6)
                        for e in range(2):
                            nc.scalar.activation(slot1[0:64, s, e:SH:2, :], pj[64 * e:64 * e + 64, :, :],
                                                 ACT.Copy).then_inc(qh_done, 1)
                    if refill_g is not None:
                        act.wait_ge(w_staged[s], 16 * (refill_g + 1))
                        nc.scalar.activation(wh[:, s], w_stage[:, s], ACT.Copy).then_inc(w_hi, 1)

            content_hi(0)
            act.wait_ge(init_done, 6)
            for zeroed in slot_zeroed:
                act.wait_ge(zeroed, 1)
            body(0, True, False, True, None)
            with act.Fori(1, B - 1) as b:
                body(b, False, False, True, None)
            body(B - 1, False, False, True, 1)
            with act.Fori(1, G - 1) as g:
                with act.Fori(0, B - 1) as b:
                    body(g * B + b, False, False, True, None)
                body(g * B + (B - 1), False, False, True, g + 1)
            with act.Fori(0, B - 1) as b:
                body(b + (G - 1) * B, False, False, True, None)
            body(NT - 1, False, False, False, None)
            body(NT, False, True, False, None)
            act.wait_ge(av_done, NT * NS)
            act.wait_ge(o_stored, 16 * NT)
            nc.scalar.activation(o_sb[:, :], ob[:, 0, :], ACT.Copy).then_inc(o_evac, 1)

        @block.vector
        def _(dve):
            def content_lo(tt):
                dve.wait_ge(ct_hi, tt + 1)
                for lo, piece in ((0, 1), (64, 2)):
                    nc.vector.tensor_tensor(content[lo:lo + 64, piece, :], ob[lo:lo + 64, 1, :],
                                            content[lo:lo + 64, 0, :], ALU.subtract).then_inc(ct_lo, 1)

            def body(t, first, last, more):
                for s in range(NS if not last else 2):
                    u = t * NS + s
                    if not first or s >= 2:
                        sv = (s + 2) % NS
                        dve.wait_ge(mt_done, u - 1)
                        nc.vector.tensor_copy(mrow[:, sv, :], sx[0:SH * 2, 0, 0:128]).then_inc(mrow_ready, 1)
                    if (not first or s >= 1) and not (last and s >= 1):
                        dve.wait_ge(qh_done, 2 * u)
                        sv = (s + 3) % NS
                        nc.vector.tensor_copy(slot2[0:64, sv, :, :], slot1[0:64, sv, :, :]).then_inc(s2_done, 1)
                    if (not first or s >= 1) and not (last and s >= 1):
                        v, sv = u - 1, (s + 3) % NS
                        for j in range(SH):
                            if j == 2 and s == NS - 1 and more:
                                content_lo(t + 1)
                            dve.wait_ge(smax_done, v * SH + j + 1)
                            nc.vector.tensor_reduce(mx[:, sv, 2 * j:2 * j + 2],
                                                    sx[:, j % 2, :].rearrange("p (a k) -> p a k", a=2),
                                                    axis=AX.X, op=ALU.max).then_inc(max_done, 1)
                    if not last:
                        for e in range(2):
                            dve.wait_ge(qh_done, 2 * u + e + 1)
                            nc.vector.tensor_tensor(slot2[64:128, s, e:SH:2, :], pj[64 * e:64 * e + 64, :, :],
                                                    slot1[0:64, s, e:SH:2, :], ALU.subtract).then_inc(ql_done, 1)

            nc.vector.memset(slot1[:, 0:2, :, :].bitcast(F32), 0.0).then_inc(slot_zeroed[0], 1)
            content_lo(0)
            iterations(dve, body)

        @block.tensor
        def _(pe):
            def content_product(tt):
                pe.wait_ge(up_ready, tt // B + 1)
                nc.tensor.matmul(ob[:, 1, :], up[:, :], cT[:, bass.ds((tt % B) * S, S)],
                                 start=True, stop=True).then_inc(content_done, 1)

            def transpose_max(s, v):
                pe.wait_ge(max_done, v * SH + SH)
                nc.tensor.transpose(sx[0:SH * 2, 0, 0:128], mx[:, s, :], ident[:, :]).then_inc(mt_done, 1)

            def scores(s, v, first, between=None):
                pe.wait_ge(ql_done, 2 * v + 2)
                pe.wait_ge(s2_done, v + 1)
                for kt in range(2):
                    ks = slice(kt * 128, kt * 128 + 128)
                    if not first:
                        pe.wait_ge(exp_done, 2 * v - 1 + kt)
                    for n, (kk, q, rows) in enumerate(((k1[0:KC + 1, s, ks], slot1, KC + 1), (k2[:, ks], slot2, 128))):
                        for hf in range(2):
                            last = nc.tensor.matmul(st[:, kt, 2 * hf:2 * hf + 2, :], kk,
                                                    q[0:rows, s, 2 * hf:2 * hf + 2, :],
                                                    start=(n == 0), stop=(n == 1))
                    last.then_inc(st_done, 1)
                    if kt == 0 and between is not None:
                        transpose_max(*between)

            def row_scores(s, v, j, first):
                if j >= 2 or not first:
                    pe.wait_ge(max_done, v * SH + j - 1)
                for qt in range(2):
                    last = nc.tensor.matmul(sx[:, j % 2, qt * S:(qt + 1) * S],
                                            slot1[0:KC, s, j, qt * 128:qt * 128 + 128], k1[0:KC, s, :],
                                            start=True, stop=True)
                last.then_inc(smax_done, 1)

            def project(t, s, bs):
                for p in range(2):
                    for k in range(KD):
                        for n, (w, xx) in enumerate(((wh, xh), (wh, xl), (wl, xh))):
                            last = nc.tensor.matmul(pj[:, p, :], w[:, s, k, 128 * p:128 * p + 128], xx[:, k, bs],
                                                    start=(k == 0 and n == 0), stop=(k == KD - 1 and n == 2))
                last.then_inc(proj_done, 1)

            def project_step(t, s, u, bs, very_first):
                pe.wait_ge(w_ready, (t // B) * NS + s + 1)
                if not very_first:
                    pe.wait_ge(ql_done, 2 * u)
                project(t, s, bs)

            def values(s, v):
                for kt in range(2):
                    for j in range(SH):
                        last = nc.tensor.matmul(ob[32 * j:32 * j + 32, 0, :], vx[:, s, kt, j, :], probs[:, kt, j, :],
                                                start=(s == 0 and kt == 0), stop=(s == NS - 1 and kt == 1),
                                                tile_position=(0, 32 * j))
                last.then_inc(av_done, 1)

            def body(t, first, last, more):
                bs = bass.ds((t % B) * S, S)
                for s in range(NS if not last else 3):
                    u = t * NS + s
                    has_v3 = not first or s >= 3
                    has_v1 = (not first or s >= 1) and not (last and s >= 1)
                    s3, s1 = (s + 1) % NS, (s + 3) % NS
                    if has_v3:
                        v = u - 3
                        tv = t if s == 3 else t - 1
                        pe.wait_ge(mrow_in[s3], 16 * (tv + 1))
                        pe.wait_ge(k2_ready, tv + 1)
                        scores(s3, v, first, ((s + 2) % NS, u - 2) if not last or s < 2 else None)
                    elif first and s == 2:
                        transpose_max(0, 0)
                    if s == NS - 1:
                        if not first:
                            pe.wait_ge(o_evac, t)
                        if more:
                            content_product(t + 1)
                    if first and s == 1:
                        project_step(t, s, u, bs, False)
                    if has_v1:
                        v = u - 1
                        tv = t if s >= 1 else t - 1
                        pe.wait_ge(qh_done, 2 * v + 2)
                        if first and s == 1:
                            pe.wait_ge(init_done, 6)
                            for zeroed in slot_zeroed:
                                pe.wait_ge(zeroed, 1)
                            pe.wait_ge(ct_lo, 2)
                        pe.wait_ge(ct_in[s1], 80 * (tv + 1))
                        pe.wait_ge(k_ready, v + 1)
                        if not (first and s == 1):
                            pe.wait_ge(mrow_ready, v)
                        row_scores(s1, v, 0, first and s == 1)
                        row_scores(s1, v, 1, first and s == 1)
                    if not last and not (first and s == 1):
                        project_step(t, s, u, bs, first and s == 0)
                    if has_v1:
                        row_scores(s1, u - 1, 2, False)
                        row_scores(s1, u - 1, 3, False)
                    if has_v3:
                        v = u - 3
                        pe.wait_ge(exp_done, 2 * v + 2)
                        pe.wait_ge(vx_ready, v + 1)
                        if s == NS - 1 and more:
                            pe.wait_ge(ct_lo, 2 * (t + 2))
                        values(s3, v)

            content_product(0)
            iterations(pe, body)


def finish(nc, sb, sem, passed, x_tok, xh, xl, o_dram, wo, w1qT, a1T, b1T, w3qT, a3T, b3T, w2qT, a2T, b2T, out_tok):
    ctx = ExitStack()
    with ctx:
        NR = len(FR)
        w13h = sb(ctx, "w13h", [128, 2, FF], F32R)
        w13l = sb(ctx, "w13l", [128, 2, FF], F32R)
        w2h = sb(ctx, "w2h", [128, NR, D], F32R)
        w2l = sb(ctx, "w2l", [128, NR, D], F32R)
        woh = sb(ctx, "woh", [128, KD, D], F32R)
        wol = sb(ctx, "wol", [128, KD, D], F32R)
        b13 = sb(ctx, "b13", [96, 2, FF], F32R)
        lr = sb(ctx, "lr", [96, T], F32R)
        sh = sb(ctx, "sh", [128, T], F32R)
        sl = sb(ctx, "sl", [128, T], F32R)
        a2 = sb(ctx, "a2", [128, NR, 4, 32])
        b2 = sb(ctx, "b2", [128, D])
        num = sb(ctx, "num", [128, KD, CH])
        den = sb(ctx, "den", [128, KD, CH])
        num_loaded = sem("num_loaded")
        den_loaded = sem("den_loaded")
        recip = sem("recip_done")

        setup_ffn(nc, sb, sem, passed, xh, xl, wo, w1qT, a1T, b1T, w3qT, a3T, b3T, w2qT, a2T, b2T,
                  w13h, w13l, w2h, w2l, woh, wol, b13, lr, sh, sl, a2, b2, o_dram, num, den, num_loaded, den_loaded, recip)
        ffn_and_output(nc, sb, sem, passed, x_tok, xh, xl, o_dram, w13h, w13l, w2h, w2l, woh, wol, b13, lr, sh, sl,
                       a2, b2, num, den, num_loaded, den_loaded, recip, out_tok)


def setup_ffn(nc, sb, sem, passed, xh, xl, wo, w1qT, a1T, b1T, w3qT, a3T, b3T, w2qT, a2T, b2T,
              w13h, w13l, w2h, w2l, woh, wol, b13, lr, sh, sl, a2, b2, o_dram, num, den, num_loaded, den_loaded, recip):
    NR = len(FR)
    FH = FF // 2
    ctx = ExitStack()
    with ctx:
        raw13 = sb(ctx, "raw13", [128, 2, FF])
        raw2 = sb(ctx, "raw2", [128, NR, D])
        rawo = sb(ctx, "rawo", [128, KD, D])
        rawb = sb(ctx, "rawb", [96, 2, FH])
        rawa = sb(ctx, "rawa", [128, KD, 2 * RANK])
        la = sb(ctx, "la", [128, KD, 96])
        lah = sb(ctx, "lah", [128, KD, 96], F32R)
        lal = sb(ctx, "lal", [128, KD, 96], F32R)
        one = sb(ctx, "one", [128, 128])
        oner = sb(ctx, "oner", [128, 128], F32R)
        lrt = sb(ctx, "lrt", [96, CH], F32R)
        sump = [ctx.enter_context(nc.psum_tensor(f"sump{i}", [128, CH], F32)) for i in range(2)]
        lp = [ctx.enter_context(nc.psum_tensor(f"lp{i}", [96, CH], F32)) for i in range(2)]

        loaded = [sem(f"fl{i}") for i in range(5)]
        zeroed = sem("f_zeroed")
        one_zero = sem("f_one_zero")
        la_zero = sem("f_la_zero")
        pads = sem("f_pads")
        eye = sem("f_eye")
        la_ready = sem("f_la_ready")
        la_hi = sem("f_la_hi")
        la_split = sem("f_la_split")
        hi = sem("f_hi")
        lo = sem("f_lo")
        sum_done = sem("f_sum_done")
        lp_done = sem("f_lp_done")
        sh_done = sem("f_sh_done")
        sl_done = sem("f_sl_done")
        lrh_done = sem("f_lrh_done")
        lr_done = sem("f_lr_done")
        b_zero = sem("f_b_zero")
        b_hi = sem("f_b_hi")
        b_lo = sem("f_b_lo")
        block = ctx.enter_context(nc.Block())

        @block.sync
        def _(sp):
            def load_b(hf):
                for r in (0, 32, 64):
                    sp.dma_start(rawb[r:r + RANK, 0, :], b1T[:, hf * FH:(hf + 1) * FH]).then_inc(loaded[4], 16)
                    sp.dma_start(rawb[r + RANK:r + 2 * RANK, 1, :], b3T[:, hf * FH:(hf + 1) * FH]).then_inc(loaded[4], 16)

            sp.dma_start(rawa[:, :, 0:RANK], a1T.rearrange("(k p) n -> p k n", p=128)).then_inc(loaded[0], 16)
            sp.dma_start(rawa[:, :, RANK:2 * RANK], a3T.rearrange("(k p) n -> p k n", p=128)).then_inc(loaded[0], 16)
            sp.dma_start(raw13[:, 0, :], w1qT).then_inc(loaded[1], 16)
            sp.dma_start(raw13[:, 1, :], w3qT).then_inc(loaded[1], 16)
            load_attention(sp, o_dram, den, 1, 0, den_loaded)
            sp.wait_ge(b_zero, 1)
            load_b(0)
            sp.dma_start(raw2[:, 0:2, :], w2qT[0:256, :].rearrange("(k p) n -> p k n", p=128)).then_inc(loaded[2], 16)
            sp.dma_start(raw2[0:FR[2], 2, :], w2qT[256:FB, :]).then_inc(loaded[2], 16)
            sp.dma_start(rawo[:, :, :], wo.rearrange("(k p) n -> p k n", p=128)).then_inc(loaded[2], 16)
            load_attention(sp, o_dram, num, 0, 0, num_loaded)
            sp.wait_ge(zeroed, 2)
            for r in range(NR):
                sp.dma_start(a2[0:FR[r], r, :, 0:RANK],
                             a2T.rearrange("(j p) n -> p j n", j=4)[128 * r:128 * r + FR[r], :, :]).then_inc(pads, 16)
            for j in range(4):
                sp.dma_start(b2[32 * j:32 * j + RANK, :], b2T).then_inc(pads, 16)
            sp.wait_ge(b_lo, 1)
            load_b(1)
            sp.wait_ge(pads, 16 * 7)

        @block.gpsimd
        def _(pool):
            def b_lo_part(hf):
                pool.wait_ge(b_hi, hf + 1)
                fs = slice(hf * FH, (hf + 1) * FH)
                nc.gpsimd.tensor_tensor(b13[32:64, :, fs], rawb[32:64, :, :], b13[32:64, :, fs],
                                        ALU.subtract).then_inc(b_lo, 1)

            nc.gpsimd.memset(one[:, :], 0.0).then_inc(one_zero, 1)
            pool.wait_ge(one_zero, 1)
            nc.gpsimd.affine_select(out=one[:, :], in_=one[:, :], compare_op=ALU.not_equal, fill=1.0,
                                    base=0, pattern=[[-1, 128]], channel_multiplier=1).then_inc(eye, 1)
            nc.gpsimd.memset(la[:, :, :], 0.0).then_inc(la_zero, 1)
            pool.wait_ge(la_zero, 1)
            pool.wait_ge(loaded[0], 32)
            for c in (0, 32, 64):
                nc.gpsimd.tensor_copy(la[:, :, c:c + 2 * RANK], rawa[:, :, :]).then_inc(la_ready, 1)
            nc.gpsimd.memset(rawb[:, :, :], 0.0).then_inc(b_zero, 1)
            nc.gpsimd.memset(a2[:, :, :, :], 0.0).then_inc(zeroed, 1)
            nc.gpsimd.memset(b2[:, :], 0.0).then_inc(zeroed, 1)
            pool.wait_ge(hi, 1)
            nc.gpsimd.tensor_tensor(w13l[:, :, :], raw13[:, :, :], w13h[:, :, :], ALU.subtract).then_inc(lo, 1)
            pool.wait_ge(lo, 1)
            b_lo_part(0)
            pool.wait_ge(b_lo, 1)
            pool.wait_ge(hi, 2)
            nc.gpsimd.tensor_tensor(w2l[:, 0:2, :], raw2[:, 0:2, :], w2h[:, 0:2, :], ALU.subtract)
            nc.gpsimd.tensor_tensor(w2l[0:FR[2], 2, :], raw2[0:FR[2], 2, :], w2h[0:FR[2], 2, :], ALU.subtract)
            nc.gpsimd.tensor_tensor(wol[:, :, :], rawo[:, :, :], woh[:, :, :], ALU.subtract).then_inc(lo, 1)
            pool.wait_ge(lo, 2)
            b_lo_part(1)

        @block.scalar
        def _(act):
            act.wait_ge(eye, 1)
            nc.scalar.activation(oner[:, :], one[:, :], ACT.Copy).then_inc(la_hi, 1)
            act.wait_ge(la_ready, 3)
            nc.scalar.activation(lah[:, :, :], la[:, :, :], ACT.Copy).then_inc(la_hi, 1)

            def b_hi_part(hf):
                act.wait_ge(loaded[4], 96 * (hf + 1))
                nc.scalar.activation(b13[:, :, hf * FH:(hf + 1) * FH], rawb[:, :, :], ACT.Copy).then_inc(b_hi, 1)

            act.wait_ge(loaded[1], 32)
            nc.scalar.activation(w13h[:, :, :], raw13[:, :, :], ACT.Copy).then_inc(hi, 1)
            def chunk(c):
                cs = slice(c * CH, (c + 1) * CH)
                act.wait_ge(sum_done, c + 1)
                nc.scalar.activation(sh[:, cs], sump[c % 2][:, :], ACT.Copy).then_inc(sh_done, 1)
                act.wait_ge(lp_done, c + 1)
                wait(act, lr_done, c)
                nc.scalar.activation(lr[0:64, cs], lp[c % 2][0:64, :], ACT.Copy, scale=0.5)
                nc.scalar.activation(lrt[64:96, :], lp[c % 2][64:96, :], ACT.Copy, scale=0.5).then_inc(lrh_done, 1)

            chunk(0)
            b_hi_part(0)
            chunk(1)
            act.wait_ge(loaded[2], 48)
            nc.scalar.activation(w2h[:, 0:2, :], raw2[:, 0:2, :], ACT.Copy)
            nc.scalar.activation(w2h[0:FR[2], 2, :], raw2[0:FR[2], 2, :], ACT.Copy)
            nc.scalar.activation(woh[:, :, :], rawo[:, :, :], ACT.Copy).then_inc(hi, 1)
            chunk(2)
            chunk(3)
            b_hi_part(1)

        @block.vector
        def _(dve):
            dve.wait_ge(la_hi, 2)
            nc.vector.tensor_tensor(lal[:, :, :], la[:, :, :], lah[:, :, :], ALU.subtract).then_inc(la_split, 1)
            def chunk(c):
                cs = slice(c * CH, (c + 1) * CH)
                dve.wait_ge(sh_done, c + 1)
                nc.vector.tensor_tensor(sl[:, cs], sump[c % 2][:, :], sh[:, cs], ALU.subtract).then_inc(sl_done, 1)
                dve.wait_ge(lrh_done, c + 1)
                nc.vector.scalar_tensor_tensor(out=lr[64:96, cs], in0=lp[c % 2][64:96, :], scalar=0.5, in1=lrt[64:96, :],
                                               op0=ALU.mult, op1=ALU.subtract).then_inc(lr_done, 1)

            def reciprocals(kts):
                for kt in kts:
                    nc.vector.reciprocal(den[:, kt, :], den[:, kt, :]).then_inc(recip, 1)

            chunk(0)
            dve.wait_ge(den_loaded, 16 * KD)
            reciprocals((0,))
            chunk(1)
            reciprocals((1,))
            chunk(2)
            reciprocals((2,))
            chunk(3)
            reciprocals((3,))

        @block.tensor
        def _(pe):
            pe.wait_ge(la_hi, 1)
            def chunk(c, first=False):
                cs = slice(c * CH, (c + 1) * CH)
                wait(pe, sl_done, c - 1)
                for k in range(KD):
                    for xx in (xh, xl):
                        last = nc.tensor.matmul(sump[c % 2][:, :], oner[:, :], xx[:, k, cs],
                                                start=(k == 0 and xx is xh), stop=(k == KD - 1 and xx is xl))
                last.then_inc(sum_done, 1)
                if first:
                    pe.wait_ge(la_hi, 2)
                    pe.wait_ge(la_split, 1)
                wait(pe, lr_done, c - 1)
                for k in range(KD):
                    for n, (w, xx) in enumerate(((lah, xh), (lah, xl), (lal, xh))):
                        last = nc.tensor.matmul(lp[c % 2][:, :], w[:, k, :], xx[:, k, cs],
                                                start=(k == 0 and n == 0), stop=(k == KD - 1 and n == 2))
                last.then_inc(lp_done, 1)

            chunk(0, True)
            for c in range(1, NC):
                chunk(c)


def ffn_and_output(nc, sb, sem, passed, x_tok, xh, xl, o_dram, w13h, w13l, w2h, w2l, woh, wol, b13, lr, sh, sl,
                   a2, b2, num, den, num_loaded, den_loaded, recip, out_tok):
    NR = len(FR)
    NI = CH // 128
    MT = NR * 4
    ctx = ExitStack()
    with ctx:
        oh, ol = xh[:, :, 0:CH], xl[:, :, 0:CH]
        hh, hl = xh[:, 0:NR, CH:2 * CH], xl[:, 0:NR, CH:2 * CH]
        gate = sb(ctx, "gate", [128, 2, CH])
        hid = sb(ctx, "hid", [128, 2, 4, CH])
        hsum = sb(ctx, "hsum", [128, 2, CH])
        z = sb(ctx, "z", [128, CH])
        xt = sb(ctx, "xt", [128, 2, D])
        gt = sb(ctx, "gt", [128, 2, D])
        res = sb(ctx, "res", [128, 2, D])
        gp = [ctx.enter_context(nc.psum_tensor(f"gp{i}", [128, CH], F32)) for i in range(2)]
        up = [ctx.enter_context(nc.psum_tensor(f"up{i}", [128, CH], F32)) for i in range(2)]
        zp = ctx.enter_context(nc.psum_tensor("zp", [128, CH], F32))
        yp = [ctx.enter_context(nc.psum_tensor("yp", [128, D], F32)), zp]
        ap = [ctx.enter_context(nc.psum_tensor(f"ap{i}", [128, D], F32)) for i in range(2)]

        xt_loaded = [sem(f"xt_loaded{i}") for i in range(2)]
        on_done = sem("on_done")
        oh_done = sem("oh_done")
        ol_done = sem("ol_done")
        gate_done = sem("gate_done")
        up_done = sem("up_done")
        silu_done = sem("silu_done")
        hid_done = sem("hid_done")
        zmm_done = sem("zmm_done")
        hs_step = sem("hs_step")
        hh_done = sem("hh_done")
        hl_done = sem("hl_done")
        z_ready = sem("z_ready")
        y_done = sem("y_done")
        g_done = sem("g_done")
        a_done = sem("a_done")
        prod_done = sem("prod_done")
        res_done = sem("res_done")
        stored = [sem(f"stored{i}") for i in range(2)]
        block = ctx.enter_context(nc.Block())

        @block.sync
        def _(sp):
            def chunk(c, more):
                def load_xt(i):
                    sp.dma_start(xt[:, i % 2, :], x_tok[:, bass.ds(c * NI + i, 1), :]
                                 .rearrange("p a d -> p (a d)")).then_inc(xt_loaded[i % 2], 16)

                wait(sp, res_done, c * NI)
                load_xt(0)
                load_xt(1)
                if more:
                    hold(sp, passed, ol_done, (c + 1) * KD)
                    load_attention(sp, o_dram, den, 1, c + 1, den_loaded)
                    load_attention(sp, o_dram, num, 0, c + 1, num_loaded)
                for i in range(NI):
                    hold(sp, passed, res_done, c * NI + i + 1)
                    sp.dma_start(out_tok[:, bass.ds(c * NI + i, 1), :].rearrange("p a d -> p (a d)"),
                                 res[:, i % 2, :]).then_inc(stored[i % 2], 16)
                    if i + 2 < NI:
                        load_xt(i + 2)

            over_chunks_more(sp, chunk)
            for i in range(2):
                sp.wait_ge(stored[i], 16 * NC * NI // 2)

        @block.gpsimd
        def _(pool):
            def normalise(c, kt):
                if kt == 0:
                    hold(pool, passed, num_loaded, (c + 1) * 16 * KD)
                hold(pool, passed, recip, c * KD + kt + 1)
                nc.gpsimd.tensor_tensor(num[:, kt, :], num[:, kt, :], den[:, kt, :], ALU.mult).then_inc(on_done, 1)

            def chunk(c, more):
                for i in range(NI):
                    if more:
                        normalise(c + 1, i)
                    hold(pool, passed, xt_loaded[i % 2], 16 * (c * (NI // 2) + i // 2 + 1))
                    hold(pool, passed, prod_done, c * NI + i + 1)
                    nc.gpsimd.tensor_tensor(res[:, i % 2, :], res[:, i % 2, :], xt[:, i % 2, :], ALU.add).then_inc(res_done, 1)

            for kt in range(KD):
                normalise(0, kt)
            over_chunks_more(pool, chunk)

        def hi_part(act, c, r):
            n = FR[r]
            act.wait_ge(hs_step, (c * NR + r) * 3 + 3)
            if r == 0:
                wait(act, y_done, c * NI)
            nc.scalar.activation(hh[0:n, r, :], hsum[0:n, 1, :], ACT.Copy).then_inc(hh_done, 1)

        @block.scalar
        def _(act):
            def chunk(c):
                for m in range(MT):
                    r = m // 4
                    n = FR[r]
                    act.wait_ge(gate_done, c * MT + m + 1)
                    if m >= 2:
                        act.wait_ge(hid_done, c * MT + m - 1)
                    else:
                        wait(act, hid_done, c * MT)
                    nc.scalar.activation(gate[0:n, m % 2, :], gp[m % 2][0:n, :], ACT.Silu).then_inc(silu_done, 1)
                    if m % 4 == 0 and r > 0:
                        hi_part(act, c, r - 1)
                    if 2 <= m < 2 + KD:
                        act.wait_ge(on_done, c * KD + m - 1)
                        if m == 2:
                            wait(act, a_done, c * NI)
                        nc.scalar.activation(oh[:, m - 2, :], num[:, m - 2, :], ACT.Copy).then_inc(oh_done, 1)
                hi_part(act, c, NR - 1)
                act.wait_ge(zmm_done, (c + 1) * NR)
                nc.scalar.activation(z[:, :], zp[:, :], ACT.Copy, scale=0.5).then_inc(z_ready, 1)
                for i in range(NI):
                    act.wait_ge(y_done, c * NI + i + 1)
                    if i >= 2:
                        act.wait_ge(prod_done, c * NI + i - 1)
                    else:
                        wait(act, prod_done, c * NI)
                    nc.scalar.activation(gt[:, i % 2, :], yp[i % 2][:, :], ACT.Silu).then_inc(g_done, 1)

            over_chunks(act, chunk)

        @block.vector
        def _(dve):
            def lo_part(c, r):
                n = FR[r]
                dve.wait_ge(hh_done, c * NR + r + 1)
                nc.vector.tensor_tensor(hl[0:n, r, :], hsum[0:n, 1, :], hh[0:n, r, :],
                                        ALU.subtract).then_inc(hl_done, 1)

            def chunk(c, more):
                for m in range(MT):
                    r, j = m // 4, m % 4
                    n = FR[r]
                    dve.wait_ge(silu_done, c * MT + m + 1)
                    dve.wait_ge(up_done, c * MT + m + 1)
                    if j == 0:
                        wait(dve, zmm_done, c * NR + max(r - 1, 0))
                    nc.vector.tensor_tensor(hid[0:n, r % 2, j, :], up[m % 2][0:n, :], gate[0:n, m % 2, :],
                                            ALU.mult).then_inc(hid_done, 1)
                    if j == 1 and r > 0:
                        lo_part(c, r - 1)
                    if j >= 1:
                        dve.wait_ge(hid_done, c * MT + m + 1)
                        step = (c * NR + r) * 3 + j
                        if j > 1:
                            dve.wait_ge(hs_step, step - 1)
                        else:
                            wait(dve, hl_done, c * NR + r)
                        src = hid[0:n, r % 2, 0, :] if j == 1 else hsum[0:n, (j - 1) % 2, :]
                        nc.vector.tensor_tensor(hsum[0:n, j % 2, :], src, hid[0:n, r % 2, j, :], ALU.add).then_inc(hs_step, 1)
                    if m == MT - 1:
                        lo_part(c, r)
                    if 3 <= m < 3 + KD:
                        dve.wait_ge(oh_done, c * KD + m - 2)
                        nc.vector.tensor_tensor(ol[:, m - 3, :], num[:, m - 3, :], oh[:, m - 3, :],
                                                ALU.subtract).then_inc(ol_done, 1)
                for i in range(NI):
                    if more:
                        if i == 0:
                            dve.wait_ge(den_loaded, (c + 2) * 16 * KD)
                        nc.vector.reciprocal(den[:, i, :], den[:, i, :]).then_inc(recip, 1)
                    dve.wait_ge(g_done, c * NI + i + 1)
                    dve.wait_ge(a_done, c * NI + i + 1)
                    if i < 2:
                        wait(dve, stored[i % 2], 16 * (c * (NI // 2)))
                    else:
                        dve.wait_ge(stored[i % 2], 16 * (c * (NI // 2) + 1))
                    nc.vector.tensor_tensor(res[:, i % 2, :], ap[i % 2][:, :], gt[:, i % 2, :],
                                            ALU.mult).then_inc(prod_done, 1)

            over_chunks_more(dve, chunk)

        @block.tensor
        def _(pe):
            def chunk(c):
                cs = bass.ds(c * CH, CH)

                def low_rank(r):
                    n = FR[r]
                    pe.wait_ge(hid_done, c * MT + 4 * r + 4)
                    if r == 0:
                        wait(pe, g_done, c * NI)
                    for j in range(4):
                        last = nc.tensor.matmul(zp[32 * j:32 * j + 32, :], a2[0:n, r, j, :], hid[0:n, r % 2, j, :],
                                                start=(r == 0), stop=(r == NR - 1), tile_position=(0, 32 * j))
                    last.then_inc(zmm_done, 1)

                def attn_out(i):
                    if i >= 2:
                        pe.wait_ge(prod_done, c * NI + i - 1)
                    else:
                        wait(pe, prod_done, c * NI)
                    for k in range(KD):
                        for n, (o, w) in enumerate(((oh, woh), (oh, wol), (ol, woh))):
                            last = nc.tensor.matmul(ap[i % 2][:, :], o[:, k, i * 128:(i + 1) * 128], w[:, k, :],
                                                    start=(k == 0 and n == 0), stop=(k == KD - 1 and n == 2))
                    last.then_inc(a_done, 1)

                for m in range(MT):
                    r, j = m // 4, m % 4
                    n = FR[r]
                    lo = FB * j + 128 * r
                    for w, (dst, done) in enumerate(((gp, gate_done), (up, up_done))):
                        if m >= 2:
                            pe.wait_ge(hid_done, c * MT + m - 1)
                        else:
                            wait(pe, hid_done, c * MT)
                        nc.tensor.matmul(dst[m % 2][0:n, :], w13h[:, w, lo:lo + n], sh[:, cs], start=True, stop=False)
                        nc.tensor.matmul(dst[m % 2][0:n, :], w13h[:, w, lo:lo + n], sl[:, cs], start=False, stop=False)
                        nc.tensor.matmul(dst[m % 2][0:n, :], w13l[:, w, lo:lo + n], sh[:, cs], start=False, stop=False)
                        nc.tensor.matmul(dst[m % 2][0:n, :], b13[:, w, lo:lo + n], lr[:, cs],
                                         start=False, stop=True).then_inc(done, 1)
                    if m in (5, 9):
                        low_rank(r - 1)
                pe.wait_ge(ol_done, (c + 1) * KD)
                attn_out(0)
                low_rank(NR - 1)
                attn_out(1)
                pe.wait_ge(hl_done, (c + 1) * NR)
                pe.wait_ge(z_ready, c + 1)
                for i in range(NI):
                    ts = slice(i * 128, (i + 1) * 128)
                    if i >= 2:
                        pe.wait_ge(g_done, c * NI + i - 1)
                    else:
                        wait(pe, g_done, c * NI)
                    for r in range(NR):
                        n = FR[r]
                        for q, (h, w) in enumerate(((hh, w2h), (hh, w2l), (hl, w2h))):
                            nc.tensor.matmul(yp[i % 2][:, :], h[0:n, r, ts], w[0:n, r, :],
                                             start=(r == 0 and q == 0), stop=False)
                    nc.tensor.matmul(yp[i % 2][:, :], z[:, ts], b2[:, :], start=False, stop=True).then_inc(y_done, 1)
                    if 1 <= i < NI - 1:
                        attn_out(i + 1)

            over_chunks(pe, chunk)


_INS = ["x", "Wq_down", "Wq_up", "Wq_rope", "Wkv_down", "Wk_up", "Wv_up", "Wk_rope", "Wo"]
_FFN = ["w1q", "a1", "b1", "w3q", "a3", "b3", "w2q", "a2", "b2"]


def kernel(**inputs):
    import numpy as _np
    import concourse.bacc as _bacc
    from concourse import mybir as _mybir
    from concourse.bass_utils import run_bass_kernel_spmd as _run

    nc = _bacc.Bacc("TRN2", target_bir_lowering=False, num_devices=1)
    arrays, args = {}, {}

    def give(name, a):
        a = _np.ascontiguousarray(a)
        arrays[name] = a
        args[name] = nc.dram_tensor(name, a.shape, _mybir.dt.from_np(a.dtype), kind="ExternalInput").ap()

    for name in _INS:
        a = _np.asarray(inputs["L0_attn_" + name])
        if name == "Wq_rope":
            a = a.reshape(KD, 128, G, SH, NS, ROPE).transpose(2, 4, 1, 0, 3, 5).reshape(G, NS, 128, KD * SH * ROPE)
        elif name in ("Wq_up", "Wk_up"):
            a = a.reshape(LAT, G, SH, NS, HD).transpose(0, 1, 3, 2, 4).reshape(LAT, H * HD)
        give("in_" + name, a)
    for name in _FFN:
        give("in_" + name + "T", _np.asarray(inputs["L0_ffn_" + name]).T)
    shape = inputs["L0_attn_x"].shape
    out = nc.dram_tensor("out_dram", shape, _mybir.dt.float32, kind="ExternalOutput").ap()
    a = args
    attn_ffn_layer(nc, a["in_x"], a["in_Wq_down"], a["in_Wq_up"], a["in_Wq_rope"], a["in_Wkv_down"],
                   a["in_Wk_up"], a["in_Wv_up"], a["in_Wk_rope"], a["in_Wo"],
                   a["in_w1qT"], a["in_a1T"], a["in_b1T"], a["in_w3qT"], a["in_a3T"], a["in_b3T"],
                   a["in_w2qT"], a["in_a2T"], a["in_b2T"], out)
    r = _run(nc, [arrays], core_ids=[0])
    return r.results[0]["out_dram"]
```
